# Optimizing a Trainium2 kernel written in Bass

```python
import numpy as np
import jax
import jax.numpy as jnp

def _softmax(x, axis=-1):
    return jax.nn.softmax(x, axis=axis)

def _gelu(x):
    return jax.nn.gelu(x, approximate=True)

def _silu(x):
    return jax.nn.silu(x)

def _sigmoid(x):
    return jax.nn.sigmoid(x)

def _layernorm(x, axis=-1, eps=1e-05):
    m = jnp.mean(x, axis=axis, keepdims=True)
    v = jnp.var(x, axis=axis, keepdims=True)
    return (x - m) / jnp.sqrt(v + eps)

def _scatter_add(tgt, idx, src, axis=0):
    return tgt.at[idx].add(src)

def _segment_sum(src, seg, n):
    return jax.ops.segment_sum(src, seg, n)
kernel_name = 'mk_vit_tower_postln_d2_tok_img1024_r4_f86a9c'

def setup_inputs(seed: int=0):
    np.random.seed(seed)
    _w = jnp.asarray

    def _rec_inputs():
        import jax
        import jax.numpy as jnp
        _rk = jax.random.key(seed)
        x = -0.00016672 + 0.999947 * jax.random.normal(jax.random.fold_in(_rk, 1), (32, 3, 96, 96), jnp.float32)
        return x
    x = _rec_inputs()

    def _L0_tok_setup():
        import jax, jax.numpy as jnp
        import numpy as np
        EMBED_DIM = 256
        IMAGE_SIZE = 96
        CHANNELS = 3
        PATCH = 16
        NUM_PATCHES = (IMAGE_SIZE // PATCH) ** 2
        PATCH_DIM = PATCH * PATCH * CHANNELS

        def _patchify(x, patch):
            B, C, H, W = x.shape
            hp, wp = (H // patch, W // patch)
            x = x.reshape(B, C, hp, patch, wp, patch)
            x = x.transpose(0, 2, 4, 1, 3, 5)
            return x.reshape(B, hp * wp, C * patch * patch)
        key = jax.random.key(seed)
        k_x, k_w, k_b, k_cls, k_pos = jax.random.split(key, 5)
        x = jax.random.normal(k_x, (64, CHANNELS, IMAGE_SIZE, IMAGE_SIZE), dtype=jnp.float32)
        W = jax.random.normal(k_w, (EMBED_DIM, PATCH_DIM), dtype=jnp.float32) / np.sqrt(PATCH_DIM)
        b = jax.random.normal(k_b, (EMBED_DIM,), dtype=jnp.float32) * 0.01
        cls_token = jax.random.normal(k_cls, (1, 1, EMBED_DIM), dtype=jnp.float32)
        pos_embedding = jax.random.normal(k_pos, (1, 1 + NUM_PATCHES, EMBED_DIM), dtype=jnp.float32)
        return {'x': x, 'W': W, 'b': b, 'cls_token': cls_token, 'pos_embedding': pos_embedding}
    _L0_tok_all = _L0_tok_setup()
    _L0_tok_in = {k: v for k, v in _L0_tok_all.items() if k in ('W', 'b', 'cls_token', 'pos_embedding')}
    del _L0_tok_all

    def _L0_attn_setup():
        import jax, jax.numpy as jnp
        import numpy as np
        D_MODEL = 256
        NUM_HEADS = 16
        DK = D_MODEL // NUM_HEADS
        key = jax.random.key(seed)
        kx, kq, kk, kv, ko = jax.random.split(key, 5)
        B, S = (4, 512)
        bound = float(np.sqrt(6.0 / (D_MODEL + D_MODEL)))
        uni = lambda k: jax.random.uniform(k, (D_MODEL, D_MODEL), jnp.float32, -bound, bound)
        return {'x': jax.random.normal(kx, (B, S, D_MODEL), jnp.float32), 'q_heads': uni(kq), 'k_heads': uni(kk), 'v_heads': uni(kv), 'output_proj': uni(ko)}
    _L0_attn_all = _L0_attn_setup()
    _L0_attn_in = {k: v for k, v in _L0_attn_all.items() if k in ('q_heads', 'k_heads', 'v_heads', 'output_proj')}
    del _L0_attn_all

    def _L0_ffn_setup():
        import jax, jax.numpy as jnp
        import numpy as np
        B, T, D, E, TOP_K = (4, 1024, 256, 8, 2)
        CAPACITY_FACTOR = 1.5
        key = jax.random.key(seed)
        k1, k2, k3 = jax.random.split(key, 3)
        x = jax.random.normal(k1, (B, T, D), dtype=jnp.float32)
        Wr = jax.random.normal(k2, (E, D), dtype=jnp.float32) * 0.02
        We = jax.random.normal(k3, (E, D, D), dtype=jnp.float32) * 0.02
        return {'x': x, 'Wr': Wr, 'We': We}
    _L0_ffn_all = _L0_ffn_setup()
    _L0_ffn_in = {k: v for k, v in _L0_ffn_all.items() if k in ('Wr', 'We')}
    del _L0_ffn_all

    def _L1_attn_setup():
        import jax, jax.numpy as jnp
        import numpy as np
        import math
        B, T, C = (4, 512, 256)
        H, DQK, DV = (16, 64, 64)
        key = jax.random.key(seed)
        k1, k2, k3, k4, k5 = jax.random.split(key, 5)
        x_q = jax.random.normal(k1, (B, T, C), dtype=jnp.float32)
        w_q = jax.random.normal(k2, (H, DQK, C), dtype=jnp.float32) / math.sqrt(C)
        w_k = jax.random.normal(k3, (H, DQK, C), dtype=jnp.float32) / math.sqrt(C)
        w_v = jax.random.normal(k4, (H, DV, C), dtype=jnp.float32) / math.sqrt(C)
        w_o = jax.random.normal(k5, (DV * H, C), dtype=jnp.float32) / math.sqrt(C)
        return {'x_q': x_q, 'w_q': w_q, 'w_k': w_k, 'w_v': w_v, 'w_o': w_o}
    _L1_attn_all = _L1_attn_setup()
    _L1_attn_in = {k: v for k, v in _L1_attn_all.items() if k in ('w_q', 'w_k', 'w_v', 'w_o')}
    del _L1_attn_all

    def _L1_ffn_setup():
        import jax, jax.numpy as jnp
        import numpy as np
        EPS = 1e-05

        def act_quant(x):
            scale = 127.0 / jnp.clip(jnp.max(jnp.abs(x), axis=-1, keepdims=True), EPS, None)
            q = jnp.clip(jnp.round(x * scale), -128.0, 127.0) / scale
            return x + jax.lax.stop_gradient(q - x)

        def weight_quant(w):
            scale = 1.0 / jnp.clip(jnp.mean(jnp.abs(w)), EPS, None)
            q = jnp.clip(jnp.round(w * scale), -1.0, 1.0) / scale
            return w + jax.lax.stop_gradient(q - w)

        def bitlinear(x, w):
            return act_quant(x) @ weight_quant(w).T
        key = jax.random.key(seed)
        k1, k2, k3, k4 = jax.random.split(key, 4)
        H, I = (256, 1024)
        B, S = (4, 1024)
        init = 0.02
        x = jax.random.normal(k1, (B, S, H), dtype=jnp.float32)
        w_gate = jax.random.normal(k2, (I, H), dtype=jnp.float32) * init
        w_up = jax.random.normal(k3, (I, H), dtype=jnp.float32) * init
        w_down = jax.random.normal(k4, (H, I), dtype=jnp.float32) * init
        return {'x': x, 'w_gate': w_gate, 'w_up': w_up, 'w_down': w_down}
    _L1_ffn_all = _L1_ffn_setup()
    _L1_ffn_in = {k: v for k, v in _L1_ffn_all.items() if k in ('w_gate', 'w_up', 'w_down')}
    del _L1_ffn_all
    return {'x': x, 'L0_tok_W': _L0_tok_in['W'], 'L0_tok_b': _L0_tok_in['b'], 'L0_tok_cls_token': _L0_tok_in['cls_token'], 'L0_tok_pos_embedding': _L0_tok_in['pos_embedding'], 'L0_attn_q_heads': _L0_attn_in['q_heads'], 'L0_attn_k_heads': _L0_attn_in['k_heads'], 'L0_attn_v_heads': _L0_attn_in['v_heads'], 'L0_attn_output_proj': _L0_attn_in['output_proj'], 'L0_ffn_Wr': _L0_ffn_in['Wr'], 'L0_ffn_We': _L0_ffn_in['We'], 'L1_attn_w_q': _L1_attn_in['w_q'], 'L1_attn_w_k': _L1_attn_in['w_k'], 'L1_attn_w_v': _L1_attn_in['w_v'], 'L1_attn_w_o': _L1_attn_in['w_o'], 'L1_ffn_w_gate': _L1_ffn_in['w_gate'], 'L1_ffn_w_up': _L1_ffn_in['w_up'], 'L1_ffn_w_down': _L1_ffn_in['w_down']}

def reference(x, L0_tok_W, L0_tok_b, L0_tok_cls_token, L0_tok_pos_embedding, L0_attn_q_heads, L0_attn_k_heads, L0_attn_v_heads, L0_attn_output_proj, L0_ffn_Wr, L0_ffn_We, L1_attn_w_q, L1_attn_w_k, L1_attn_w_v, L1_attn_w_o, L1_ffn_w_gate, L1_ffn_w_up, L1_ffn_w_down):
    import jax
    import jax.numpy as jnp

    def _L0_tok_ref(x, W, b, cls_token, pos_embedding):
        import jax, jax.numpy as jnp
        import numpy as np
        EMBED_DIM = 256
        IMAGE_SIZE = 96
        CHANNELS = 3
        PATCH = 16
        NUM_PATCHES = (IMAGE_SIZE // PATCH) ** 2
        PATCH_DIM = PATCH * PATCH * CHANNELS

        def _patchify(x, patch):
            B, C, H, W = x.shape
            hp, wp = (H // patch, W // patch)
            x = x.reshape(B, C, hp, patch, wp, patch)
            x = x.transpose(0, 2, 4, 1, 3, 5)
            return x.reshape(B, hp * wp, C * patch * patch)
        B = x.shape[0]
        patches = _patchify(x, PATCH)
        tokens = jnp.einsum('bnd,ed->bne', patches, W) + b
        cls = jnp.broadcast_to(cls_token, (B, 1, EMBED_DIM))
        out = jnp.concatenate([cls, tokens], axis=1)
        return out + pos_embedding

    def _L0_attn_ref(x, q_heads, k_heads, v_heads, output_proj):
        import jax, jax.numpy as jnp
        import numpy as np
        D_MODEL = 256
        NUM_HEADS = 16
        DK = D_MODEL // NUM_HEADS
        B, S, _ = x.shape

        def proj(W):
            return (x @ W.T).reshape(B, S, NUM_HEADS, DK).transpose(0, 2, 1, 3)
        q, k, v = (proj(q_heads), proj(k_heads), proj(v_heads))
        scale = 1.0 / jnp.sqrt(jnp.asarray(DK, x.dtype))
        scores = jnp.einsum('bhqd,bhkd->bhqk', q, k) * scale
        causal = jnp.triu(jnp.ones((S, S), bool), k=1)
        scores = jnp.where(causal, jnp.asarray(-jnp.inf, scores.dtype), scores)
        attn = jax.nn.softmax(scores, axis=-1)
        out = jnp.einsum('bhqk,bhkd->bhqd', attn, v)
        out = out.transpose(0, 2, 1, 3).reshape(B, S, D_MODEL)
        return out @ output_proj.T

    def _L0_ffn_ref(x, Wr, We):
        import jax, jax.numpy as jnp
        import numpy as np
        B, T, D, E, TOP_K = (4, 1024, 256, 8, 2)
        CAPACITY_FACTOR = 1.5
        Bb, Tt, Dd = x.shape
        Ee = Wr.shape[0]
        K = TOP_K
        C = int(Tt * K / Ee * CAPACITY_FACTOR) + 1
        logits = jnp.einsum('btd,ed->bte', x, Wr)
        top_vals, top_idx = jax.lax.top_k(logits, K)
        w = jax.nn.softmax(top_vals, axis=-1)
        flat_e = top_idx.reshape(Bb, Tt * K)
        oh = jax.nn.one_hot(flat_e, Ee, dtype=jnp.int32)
        pos_all = jnp.cumsum(oh, axis=1) - oh
        pos = jnp.take_along_axis(pos_all, flat_e[..., None], axis=-1)[..., 0]
        keep = pos < C
        b_idx = jnp.arange(Bb, dtype=jnp.int32)[:, None]
        dst = (b_idx * Ee + flat_e) * C + pos
        dst = jnp.where(keep, dst, Bb * Ee * C).reshape(-1)
        x_rep = jnp.repeat(x, K, axis=1).reshape(-1, Dd)
        buf = jnp.zeros((Bb * Ee * C, Dd), dtype=x.dtype).at[dst].add(x_rep, mode='drop')
        expert_in = buf.reshape(Bb, Ee, C, Dd)
        expert_out = jnp.einsum('becd,edf->becf', expert_in, We)
        gathered = jnp.take(expert_out.reshape(Bb * Ee * C, Dd), dst, axis=0, mode='fill', fill_value=0.0)
        gathered = gathered.reshape(Bb, Tt, K, Dd)
        out = jnp.einsum('btk,btkd->btd', w, gathered)
        return out

    def _L1_attn_ref(x_q, w_q, w_k, w_v, w_o):
        import jax, jax.numpy as jnp
        import numpy as np
        import math
        B, T, C = (4, 512, 256)
        H, DQK, DV = (16, 64, 64)
        q = jnp.einsum('ntc,hdc->nhtd', x_q, w_q)
        k = jnp.einsum('ntc,hdc->nhtd', x_q, w_k)
        v = jnp.einsum('ntc,hdc->nhtd', x_q, w_v)
        a = jnp.einsum('nhtd,nhsd->nhts', q, k) / math.sqrt(q.shape[3])
        t = a.shape[2]
        causal_forbidden = jnp.arange(t)[:, None] < jnp.arange(t)[None, :]
        a = jnp.where(causal_forbidden[None, None], -jnp.inf, a)
        a = jax.nn.softmax(a, axis=3)
        y = jnp.einsum('nhts,nhsd->nthd', a, v).reshape(a.shape[0], t, -1)
        return y @ w_o

    def _L1_ffn_ref(x, w_gate, w_up, w_down):
        import jax, jax.numpy as jnp
        import numpy as np
        EPS = 1e-05

        def act_quant(x):
            scale = 127.0 / jnp.clip(jnp.max(jnp.abs(x), axis=-1, keepdims=True), EPS, None)
            q = jnp.clip(jnp.round(x * scale), -128.0, 127.0) / scale
            return x + jax.lax.stop_gradient(q - x)

        def weight_quant(w):
            scale = 1.0 / jnp.clip(jnp.mean(jnp.abs(w)), EPS, None)
            q = jnp.clip(jnp.round(w * scale), -1.0, 1.0) / scale
            return w + jax.lax.stop_gradient(q - w)

        def bitlinear(x, w):
            return act_quant(x) @ weight_quant(w).T
        g = bitlinear(x, w_gate)
        u = bitlinear(x, w_up)
        h = jnp.square(jax.nn.relu(g)) * u
        return bitlinear(h, w_down)
    h = _L0_tok_ref(x, L0_tok_W, L0_tok_b, L0_tok_cls_token, L0_tok_pos_embedding)
    h = _layernorm(h + _L0_attn_ref(h, L0_attn_q_heads, L0_attn_k_heads, L0_attn_v_heads, L0_attn_output_proj), axis=-1)
    h = _layernorm(h + _L0_ffn_ref(h, L0_ffn_Wr, L0_ffn_We), axis=-1)
    h = _layernorm(h + _L1_attn_ref(h, L1_attn_w_q, L1_attn_w_k, L1_attn_w_v, L1_attn_w_o), axis=-1)
    h = _layernorm(h + _L1_ffn_ref(h, L1_ffn_w_gate, L1_ffn_w_up, L1_ffn_w_down), axis=-1)
    return h

_drawn_inputs = setup_inputs


def setup_inputs(seed=0):
    import zlib

    import numpy as np

    out = dict(_drawn_inputs(seed))
    spreads = {}
    factors = {'L1_ffn_w_gate': 8.0, 'L1_ffn_w_up': 8.0, 'L1_ffn_w_down': 8.0}
    for name, (base, spread) in spreads.items():
        noise = np.random.default_rng([zlib.crc32(name.encode()), seed]).standard_normal(out[name].shape)
        drawn = base * np.exp(spread * noise) if base else spread * noise
        out[name] = jnp.asarray(drawn.astype(out[name].dtype))
    for name, factor in factors.items():
        out[name] = (out[name] * factor).astype(out[name].dtype)
    return out
```

```python
from contextlib import ExitStack

import numpy as np
import concourse.bass as bass
from concourse import mybir

F32 = mybir.dt.float32
BF16 = mybir.dt.bfloat16
U32 = mybir.dt.uint32
ALU = mybir.AluOpType
ACT = mybir.ActivationFunctionType
AX = mybir.AxisListType

B, SIDE, PATCH, CH = 32, 96, 16, 3
PER_SIDE = SIDE // PATCH
S = PER_SIDE * PER_SIDE + 1
D = 256
PD = CH * PATCH * PATCH
IMG = 3
GT = IMG * S
NG = -(-B // IMG)
KP = PD // 128
KD = D // 128
H = 16
QUADS = 4
D0 = D // H
D1 = 64
W1 = H * D1
KO = W1 // 128
E = 8
CAP = int(S * 2 / E * 1.5) + 1
FF = 1024
KF = FF // 128
EPS = 1e-5
MASKED = -1e30
ROUND = 1.5 * 2.0 ** 23

A_SLOTS = (["s0"] * QUADS + ["p0"] * QUADS + ["o0", "t0", "y0", "h1t", "logit", "moe", "place", "moe",
           "tok", "moe", "moe", "qk0", "v0"])
AHEAD = ("tok", "qk0", "v0")
B_SLOTS = (["h2t"] + ["qk1"] * 4 + ["v1"] * 2 + ["s1"] * QUADS + ["p1"] * QUADS + ["o1"] * QUADS
           + ["t1"] * 2 + ["y1", "xqt"] + ["gu"] * 4 + ["hqt"] * 2 + ["down"])
A_BANKS, B_BANKS = 3, 5
assert len(A_SLOTS) % A_BANKS == 0 and len(B_SLOTS) % B_BANKS == 0
KINDS = list(dict.fromkeys(A_SLOTS + B_SLOTS))
FILLS = {k: (A_SLOTS + B_SLOTS).count(k) for k in KINDS}


def vit_tower(nc, xp, consts, pos, cls, tokb, tokw, qk0w, v0w, o0w, wr, we, qk1w, v1w, o1w, wg, wu, wd, out):
    ctx = ExitStack()
    with ctx:
        def sb(name, shape, dt=F32):
            return ctx.enter_context(nc.sbuf_tensor(name, shape, dt))

        def sem(name):
            return ctx.enter_context(nc.semaphore(name))

        cst = sb("cst", [128, 128 + 2 * GT + 2 + E])
        ident = cst[:, 0:128]
        mask_f = cst[0:GT, 128:128 + GT]
        before_f = cst[0:GT, 128 + GT:128 + 2 * GT]
        parity = cst[:, 128 + 2 * GT:130 + 2 * GT]
        iota = cst[0:GT, 130 + 2 * GT:130 + 2 * GT + E]
        ident_b = sb("ident_b", [128, 128], BF16)
        mask_b = sb("mask_b", [GT, 4, GT], BF16)
        before_b = sb("before_b", [GT, GT], BF16)
        ones = sb("ones", [128, 128])
        eps_t = sb("eps_t", [128, 1])
        mhalf = sb("mhalf", [128, 1])
        magic_t = sb("magic_t", [128, 1])
        pos_t = sb("pos_t", [128, KD, S])
        cls_t = sb("cls_t", [128, KD])
        tokb_t = sb("tokb_t", [128, KD])
        tokw_t = sb("tokw_t", [128, KP, D])
        qk0w_t = sb("qk0w_t", [128, KD, 2 * D])
        v0w_t = sb("v0w_t", [128, KD, D])
        o0w_t = sb("o0w_t", [128, KD, D])
        wr_t = sb("wr_t", [128, KD, E])
        we_t = sb("we_t", [128, KD, E * D])
        qk1w_t = sb("qk1w_t", [128, KD, 2 * W1])
        v1w_t = sb("v1w_t", [128, KD, W1])
        o1w_t = sb("o1w_t", [128, KO, D])
        wff = sb("wff", [128, 3, 2048])
        wq = sb("wq", [128, 3, 2048], BF16)
        gate_q = wq[:, 0, :].rearrange("p (k n) -> p k n", k=KD)
        up_q = wq[:, 1, :].rearrange("p (k n) -> p k n", k=KD)
        down_q = wq[:, 2, :].rearrange("p (k n) -> p k n", k=KF)
        wabs = sb("wabs", [128, 3])
        wmean = sb("wmean", [128, 3])
        winv = sb("winv", [128, 3])
        gu_size = sb("gu_size", [128, 1])

        x_in = sb("x_in", [128, KP, GT])
        h0t = sb("h0t", [128, KD, GT])
        q0 = sb("q0", [128, 2, KD, GT])
        k0 = sb("k0", [128, KD, GT])
        v0 = sb("v0", [GT, H, D0 + 1])
        nmax0 = sb("nmax0", [GT, H])
        p0 = sb("p0", [GT, H, GT])
        p0t = sb("p0t", [GT, H, GT])
        rsum0 = sb("rsum0", [GT, H])
        o0 = sb("o0", [GT, D])
        o0t = sb("o0t", [128, KD, GT])
        h1 = sb("h1", [GT, D])
        h1t = sb("h1t", [128, KD, GT])
        logit = sb("logit", [GT, E])
        top = sb("top", [GT, 8])
        top_at = sb("top_at", [GT, 8], U32)
        top_atf = sb("top_atf", [GT, 2])
        first = sb("first", [GT, E])
        second = sb("second", [GT, E])
        chosen = sb("chosen", [GT, E], BF16)
        gap = sb("gap", [GT, 1])
        egap = sb("egap", [GT, 1])
        esum = sb("esum", [GT, 1])
        share = sb("share", [GT, 2])
        gate1 = sb("gate1", [GT, E])
        gate2 = sb("gate2", [GT, E])
        gates = sb("gates", [GT, E])
        acc = sb("acc", [GT, D])
        h2 = sb("h2", [GT, D])
        h2t = sb("h2t", [128, KD, GT])
        q1 = sb("q1", [128, 8, GT])
        k1 = sb("k1", [128, 8, GT])
        v1 = sb("v1", [GT, H, D1 + 1])
        nmax1 = sb("nmax1", [GT, H])
        p1 = sb("p1", [GT, H, GT])
        p1t = sb("p1t", [GT, H, GT])
        rsum1 = sb("rsum1", [GT, H])
        o1 = sb("o1", [GT, W1])
        o1t = sb("o1t", [128, KO, GT])
        z1 = sb("z1", [GT, D])
        h3 = sb("h3", [GT, D])
        xmax = sb("xmax", [GT, 1])
        xtop = sb("xtop", [GT, 1])
        xinv = sb("xinv", [GT, 1])
        xscale = sb("xscale", [GT, 1])
        xstep = sb("xstep", [GT, 1])
        xstep2 = sb("xstep2", [GT, 1])
        hstep = sb("hstep", [GT, 1])
        xr = sb("xr", [GT, D])
        xq = sb("xq", [GT, D], BF16)
        xqt = sb("xqt", [128, KD, GT], BF16)
        relu = sb("relu", [GT, 2, 512])
        hid = sb("hid", [GT, 2, 512])
        hidr = sb("hidr", [GT, FF])
        hmax = sb("hmax", [GT, 2])
        htop = sb("htop", [GT, 1])
        hinv = sb("hinv", [GT, 1])
        hscale = sb("hscale", [GT, 1])
        ystep = sb("ystep", [GT, 1])
        hq = sb("hq", [GT, FF], BF16)
        hqt = sb("hqt", [128, KF, GT], BF16)
        z2 = sb("z2", [GT, D])
        res = sb("res", [GT, D])
        stats = sb("stats", [GT, 4, 6])
        mv = sb("mv", [GT, 4, 2])
        lnv = sb("lnv", [GT, 4])
        rstd = sb("rstd", [GT, 4])

        banks = [ctx.enter_context(nc.psum_tensor(f"bank{i}", [128, 512], F32)) for i in range(8)]

        full = {k: sem("full_" + k) for k in KINDS}
        drained = {k: sem("drained_" + k) for k in KINDS if k not in ("s0", "s1", "y0", "gu")}
        w_in = {k: sem("in_" + k) for k in
                ["const", "tok", "l0", "moe", "qk1", "v1", "o1", "ff"]}
        x_ready = sem("x_ready")
        out_done = sem("out_done")
        posb_sum = sem("posb_sum")
        tables_ready = sem("tables_ready")
        wabs_ready, wmean_ready = sem("wabs_ready"), sem("wmean_ready")
        wmean_clip, winv_ready, gu_sq, gu_size_ready = sem("wmean_clip"), sem("winv_ready"), sem("gu_sq"), sem("gu_size_ready")
        wclip, wround, wq_ready = sem("wclip"), sem("wround"), sem("wq_ready")
        wsum_full = sem("wsum_full")
        nmax_ready = [sem("nmax0_ready"), sem("nmax1_ready")]
        shifted = [sem("shifted0"), sem("shifted1")]
        probs = [sem("probs0"), sem("probs1")]
        rsum_ready = [sem("rsum0_ready"), sem("rsum1_ready")]
        ln_stats = [sem(f"ln_stats{i}") for i in range(4)]
        ln_var = [sem(f"ln_var{i}") for i in range(4)]
        ln_log = [sem(f"ln_log{i}") for i in range(4)]
        ln_rstd = [sem(f"ln_rstd{i}") for i in range(4)]
        h1_ready, h2_ready, h3_ready, out_ready = sem("h1_ready"), sem("h2_ready"), sem("h3_ready"), sem("out_ready")
        z1_ready, z2_ready = sem("z1_ready"), sem("z2_ready")
        top_ready, at_ready, atf_ready = sem("top_ready"), sem("at_ready"), sem("atf_ready")
        onehot_ready, chosen_ready, gap_ready, egap_ready = sem("onehot_ready"), sem("chosen_ready"), sem("gap_ready"), sem("egap_ready")
        esum_ready, share1_ready, share2_ready = sem("esum_ready"), sem("share1_ready"), sem("share2_ready")
        gate1_ready, gate2_ready = sem("gate1_ready"), sem("gate2_ready")
        xmax_ready, xtop_ready, xinv_ready, xscale_ready = sem("xmax_ready"), sem("xtop_ready"), sem("xinv_ready"), sem("xscale_ready")
        xstep2_ready, hstep_ready = sem("xstep2_ready"), sem("hstep_ready")
        xr_ready, xq_ready = sem("xr_ready"), sem("xq_ready")
        relu_ready, relu2_ready, hid_ready = sem("relu_ready"), sem("relu2_ready"), sem("hid_ready")
        hmax_ready, htop_ready, hinv_ready, hscale_ready = sem("hmax_ready"), sem("htop_ready"), sem("hinv_ready"), sem("hscale_ready")
        hidr_ready, hq_ready = sem("hidr_ready"), sem("hq_ready")

        def bank_of(stage, kind, u=0):
            slots, n, base = (A_SLOTS, A_BANKS, 0) if stage == "A" else (B_SLOTS, B_BANKS, A_BANKS)
            at = [i for i, k in enumerate(slots) if k == kind][u]
            return banks[base + at % n]

        def drained_when(kind, u, g):
            if kind in ("s0", "s1"):
                return shifted[int(kind[1])], QUADS * g + u + 1
            if kind == "y0":
                return h1_ready, g + 1
            if kind in AHEAD:
                return drained[kind], g + 2
            if kind == "moe":
                return drained["moe"], E * g + 2 * u + 2
            if kind == "gu":
                return (relu_ready, hid_ready)[u % 2], 2 * g + u // 2 + 1
            return drained[kind], FILLS[kind] * g + u + 1

        def all_drained_before(kind, g):
            per = {"moe": E, "gu": 2}.get(kind, FILLS[kind])
            return drained_when(kind, FILLS[kind] - 1, 0)[0], per * g

        def claim(pe, stage, kind, u, g):
            slots, n, base = (A_SLOTS, A_BANKS, 0) if stage == "A" else (B_SLOTS, B_BANKS, A_BANKS)
            at = [i for i, k in enumerate(slots) if k == kind][u]
            if at >= n:
                k = slots[at - n]
                pe.wait_ge(*drained_when(k, slots[:at - n].count(k), g))
            elif later(g):
                k = slots[at - n]
                if k in AHEAD:
                    pe.wait_ge(drained[k], g + 1)
                elif k == "gu":
                    u_before = slots[:at - n].count(k)
                    pe.wait_ge((relu_ready, hid_ready)[u_before % 2], 2 * g)
                else:
                    pe.wait_ge(*all_drained_before(k, g))
            return banks[base + at % n]

        def later(g):
            return not (isinstance(g, int) and g == 0)

        block = ctx.enter_context(nc.Block())

        @block.sync
        def _(sp):
            sp.dma_start(cst[:, :], consts).then_inc(w_in["const"], 16)
            sp.dma_start(pos_t[:, :, :], pos).then_inc(w_in["const"], 16)
            sp.dma_start(cls_t[:, :], cls).then_inc(w_in["const"], 16)
            sp.dma_start(tokb_t[:, :], tokb).then_inc(w_in["const"], 16)
            sp.dma_start(tokw_t[:, :, :], tokw).then_inc(w_in["tok"], 16)
            sp.dma_start(x_in[:, :, :], xp[0]).then_inc(x_ready, 16)
            sp.dma_start(qk0w_t[:, :, :], qk0w).then_inc(w_in["l0"], 16)
            sp.dma_start(v0w_t[:, :, :], v0w).then_inc(w_in["l0"], 16)
            sp.dma_start(o0w_t[:, :, :], o0w).then_inc(w_in["l0"], 16)
            sp.dma_start(wr_t[:, :, :], wr).then_inc(w_in["moe"], 16)
            sp.dma_start(we_t[:, :, :], we).then_inc(w_in["moe"], 16)
            sp.wait_ge(full["tok"], 1)
            sp.dma_start(x_in[:, :, :], xp[1]).then_inc(x_ready, 16)
            sp.dma_start(qk1w_t[:, :, :], qk1w).then_inc(w_in["qk1"], 16)
            sp.dma_start(v1w_t[:, :, :], v1w).then_inc(w_in["v1"], 16)
            sp.dma_start(o1w_t[:, :, :], o1w).then_inc(w_in["o1"], 16)
            sp.dma_start(wff[:, 0, :], wg).then_inc(w_in["ff"], 16)
            sp.dma_start(wff[:, 1, :], wu).then_inc(w_in["ff"], 16)
            sp.dma_start(wff[:, 2, :], wd).then_inc(w_in["ff"], 16)

            def store(g):
                sp.wait_ge(out_ready, g + 1)
                sp.dma_start(out[g], res[:, :]).then_inc(out_done, 16)

            with sp.Fori(1, NG - 1) as g:
                sp.wait_ge(full["tok"], g + 1)
                sp.dma_start(x_in[:, :, :], xp[g + 1]).then_inc(x_ready, 16)
                store(g - 1)
            store(NG - 2)
            store(NG - 1)
            sp.wait_ge(out_done, 16 * NG)

        @block.tensor
        def _(pe):
            def mm(o, l, r, first=True, last=True):
                return nc.tensor.matmul(o, l, r, start=first, stop=last)

            def embed(g, first=False):
                ps = bank_of("A", "tok") if first else claim(pe, "A", "tok", 0, g - 1)
                pe.wait_ge(x_ready, 16 * g + 16)
                for m in range(KD):
                    for k in range(KP):
                        last = mm(ps[:, m * GT:(m + 1) * GT], tokw_t[:, k, m * 128:(m + 1) * 128], x_in[:, k, :],
                                  k == 0, k == KP - 1)
                last.then_inc(full["tok"], 1)

            def project0(g, first=False):
                ps = bank_of("A", "qk0") if first else claim(pe, "A", "qk0", 0, g - 1)
                pe.wait_ge(drained["tok"], g + 1)
                for m in range(4):
                    for k in range(KD):
                        last = mm(ps[:, m * GT:(m + 1) * GT], qk0w_t[:, k, m * 128:(m + 1) * 128], h0t[:, k, :],
                                  k == 0, k == KD - 1)
                last.then_inc(full["qk0"], 1)
                ps = bank_of("A", "v0") if first else claim(pe, "A", "v0", 0, g - 1)
                for k in range(KD):
                    last = mm(ps[0:GT, 0:D], h0t[:, k, :], v0w_t[:, k, :], k == 0, k == KD - 1)
                last.then_inc(full["v0"], 1)

            def mask(ps):
                mm(ps[0:GT, 0:4 * GT], ident_b[0:GT, 0:GT], mask_b[:, :, :], True, False)

            def scores0(g, j):
                ps = claim(pe, "A", "s0", j, g)
                if j == 0:
                    pe.wait_ge(drained["qk0"], g + 1)
                    pe.wait_ge(drained["v0"], g + 1)
                mask(ps)
                for i in range(4):
                    r = slice(32 * j, 32 * j + 32)
                    last = mm(ps[0:GT, i * GT:(i + 1) * GT], q0[r, i % 2, i // 2, :], k0[r, i // 2, :], False, i == 3)
                last.then_inc(full["s0"], 1)

            def flip_probs(g, layer, j):
                ps = claim(pe, "AB"[layer], f"p{layer}", j, g)
                pe.wait_ge(probs[layer], QUADS * g + j + 1)
                src = (p0, p1)[layer]
                for i in range(4):
                    last = nc.tensor.transpose(ps[0:GT, i * GT:(i + 1) * GT], src[:, 4 * j + i, :], ident[0:GT, 0:GT])
                last.then_inc(full[f"p{layer}"], 1)

            def mix0(g, j):
                if j == 0:
                    claim(pe, "A", "o0", 0, g)
                ps = bank_of("A", "o0")
                pe.wait_ge(drained["p0"], QUADS * g + j + 1)
                for h in range(4 * j, 4 * j + 4):
                    last = mm(ps[0:GT, h * (D0 + 1):(h + 1) * (D0 + 1)], p0t[:, h, :], v0[:, h, :])
                if j == QUADS - 1:
                    last.then_inc(full["o0"], 1)

            def out0_flip(g):
                ps = claim(pe, "A", "t0", 0, g)
                pe.wait_ge(drained["o0"], g + 1)
                for k in range(KD):
                    last = nc.tensor.transpose(ps[:, k * GT:(k + 1) * GT], o0[:, k * 128:(k + 1) * 128], ident[0:GT, 0:GT])
                last.then_inc(full["t0"], 1)

            def out0(g):
                ps = claim(pe, "A", "y0", 0, g)
                pe.wait_ge(drained["t0"], g + 1)
                for k in range(KD):
                    mm(ps[0:GT, 0:D], o0t[:, k, :], o0w_t[:, k, :], k == 0, False)
                for k in range(KD):
                    last = mm(ps[0:GT, k * 128:(k + 1) * 128], h0t[:, k, :], ident, False, k == KD - 1)
                last.then_inc(full["y0"], 1)

            def h1_flip(g):
                ps = claim(pe, "A", "h1t", 0, g)
                pe.wait_ge(h1_ready, g + 1)
                for k in range(KD):
                    last = nc.tensor.transpose(ps[:, k * GT:(k + 1) * GT], h1[:, k * 128:(k + 1) * 128], ident[0:GT, 0:GT])
                last.then_inc(full["h1t"], 1)

            def route(g):
                ps = claim(pe, "A", "logit", 0, g)
                pe.wait_ge(drained["h1t"], g + 1)
                for k in range(KD):
                    last = mm(ps[0:GT, 0:E], h1t[:, k, :], wr_t[:, k, :], k == 0, k == KD - 1)
                last.then_inc(full["logit"], 1)

            def experts(g, u):
                ps = claim(pe, "A", "moe", u, g)
                for k in range(KD):
                    last = mm(ps[0:GT, :], h1t[:, k, :], we_t[:, k, u * 512:(u + 1) * 512], k == 0, k == KD - 1)
                last.then_inc(full["moe"], 1)

            def places(g):
                ps = claim(pe, "A", "place", 0, g)
                pe.wait_ge(chosen_ready, g + 1)
                mm(ps[0:GT, 0:E], before_b[:, :], chosen[:, :]).then_inc(full["place"], 1)

            def h2_flip(g):
                ps = claim(pe, "B", "h2t", 0, g)
                pe.wait_ge(h2_ready, g + 1)
                for k in range(KD):
                    last = nc.tensor.transpose(ps[:, k * GT:(k + 1) * GT], h2[:, k * 128:(k + 1) * 128], ident[0:GT, 0:GT])
                last.then_inc(full["h2t"], 1)

            def project1(g, u):
                ps = claim(pe, "B", "qk1", u, g)
                if u == 0:
                    pe.wait_ge(drained["h2t"], g + 1)
                for m in range(4):
                    for k in range(KD):
                        c = (4 * u + m) * 128
                        last = mm(ps[:, m * GT:(m + 1) * GT], qk1w_t[:, k, c:c + 128], h2t[:, k, :], k == 0, k == KD - 1)
                last.then_inc(full["qk1"], 1)

            def values1(g, u):
                ps = claim(pe, "B", "v1", u, g)
                for k in range(KD):
                    last = mm(ps[0:GT, :], h2t[:, k, :], v1w_t[:, k, u * 512:(u + 1) * 512], k == 0, k == KD - 1)
                last.then_inc(full["v1"], 1)

            def scores1(g, j):
                ps = claim(pe, "B", "s1", j, g)
                pe.wait_ge(drained["qk1"], 4 * g + 2 * (j // 2) + 2)
                mask(ps)
                r = slice(64 * (j % 2), 64 * (j % 2) + 64)
                for i in range(4):
                    t = 4 * (j // 2) + i
                    last = mm(ps[0:GT, i * GT:(i + 1) * GT], q1[r, t, :], k1[r, t, :], False, i == 3)
                last.then_inc(full["s1"], 1)

            def mix1(g, j):
                ps = claim(pe, "B", "o1", j, g)
                if j == 0:
                    pe.wait_ge(drained["v1"], 2 * g + 2)
                pe.wait_ge(drained["p1"], QUADS * g + j + 1)
                for i in range(4):
                    h = 4 * j + i
                    last = mm(ps[0:GT, i * (D1 + 1):(i + 1) * (D1 + 1)], p1t[:, h, :], v1[:, h, :])
                last.then_inc(full["o1"], 1)

            def out1_flip(g, u):
                ps = claim(pe, "B", "t1", u, g)
                pe.wait_ge(drained["o1"], QUADS * g + 2 * u + 2)
                for i in range(4):
                    c = (4 * u + i) * 128
                    last = nc.tensor.transpose(ps[:, i * GT:(i + 1) * GT], o1[:, c:c + 128], ident[0:GT, 0:GT])
                last.then_inc(full["t1"], 1)

            def out1(g):
                ps = claim(pe, "B", "y1", 0, g)
                pe.wait_ge(drained["t1"], 2 * g + 2)
                for k in range(KO):
                    last = mm(ps[0:GT, 0:D], o1t[:, k, :], o1w_t[:, k, :], k == 0, k == KO - 1)
                last.then_inc(full["y1"], 1)

            def xq_flip(g):
                ps = claim(pe, "B", "xqt", 0, g)[:, :].bitcast(BF16)
                pe.wait_ge(xq_ready, g + 1)
                for k in range(KD):
                    last = nc.tensor.transpose(ps[:, k * 112:k * 112 + GT], xq[:, k * 128:(k + 1) * 128], ident_b[0:GT, 0:GT])
                last.then_inc(full["xqt"], 1)

            def gate_up(g, u):
                ps = claim(pe, "B", "gu", u, g)
                if u == 0:
                    pe.wait_ge(drained["xqt"], g + 1)
                    pe.wait_ge(wq_ready, 3)
                w = (gate_q, up_q)[u % 2]
                for k in range(KD):
                    last = mm(ps[0:GT, :], xqt[:, k, :], w[:, k, (u // 2) * 512:(u // 2) * 512 + 512], k == 0, k == KD - 1)
                last.then_inc(full["gu"], 1)

            def hq_flip(g, u):
                ps = claim(pe, "B", "hqt", u, g)[:, :].bitcast(BF16)
                pe.wait_ge(hq_ready, 2 * g + u + 1)
                for i in range(4):
                    c = (4 * u + i) * 128
                    last = nc.tensor.transpose(ps[:, i * 112:i * 112 + GT], hq[:, c:c + 128], ident_b[0:GT, 0:GT])
                last.then_inc(full["hqt"], 1)

            def down(g):
                ps = claim(pe, "B", "down", 0, g)
                pe.wait_ge(drained["hqt"], 2 * g + 2)
                for k in range(KF):
                    last = mm(ps[0:GT, 0:D], hqt[:, k, :], down_q[:, k, :], k == 0, k == KF - 1)
                last.then_inc(full["down"], 1)

            def sum_sizes():
                ps = claim(pe, "B", "xqt", 0, 0)
                pe.wait_ge(wabs_ready, 3)
                mm(ps[:, 0:3], ones[:, :], wabs[:, :]).then_inc(wsum_full, 1)
                pe.wait_ge(wmean_ready, 1)

            def stage_a(g):
                embed(g, True)
                pe.wait_ge(w_in["l0"], 48)
                project0(g, True)
                pe.wait_ge(tables_ready, 6)
                for j in range(QUADS):
                    scores0(g, j)
                for j in range(QUADS):
                    flip_probs(g, 0, j)
                for j in range(QUADS):
                    mix0(g, j)
                out0_flip(g)
                out0(g)
                h1_flip(g)
                pe.wait_ge(w_in["moe"], 32)
                route(g)
                experts(g, 0)
                places(g)
                experts(g, 1)
                embed(g + 1)
                experts(g, 2)
                experts(g, 3)
                project0(g + 1)

            def stage_b(g):
                h2_flip(g)
                for u in range(4):
                    project1(g, u)
                for u in range(2):
                    values1(g, u)
                for j in range(QUADS):
                    scores1(g, j)
                for j in range(QUADS):
                    flip_probs(g, 1, j)
                for j in range(QUADS):
                    mix1(g, j)
                for u in range(2):
                    out1_flip(g, u)
                out1(g)
                xq_flip(g)
                for u in range(4):
                    gate_up(g, u)
                for u in range(2):
                    hq_flip(g, u)
                down(g)

            def both(a, b, more=True):
                h2_flip(b)
                scores0(a, 0)
                scores0(a, 1)
                project1(b, 0)
                project1(b, 1)
                scores0(a, 2)
                project1(b, 2)
                scores0(a, 3)
                project1(b, 3)
                flip_probs(a, 0, 0)
                values1(b, 0)
                flip_probs(a, 0, 1)
                values1(b, 1)
                for j in range(QUADS):
                    scores1(b, j)
                    if j < 2:
                        flip_probs(a, 0, 2 + j)
                    mix0(a, j)
                flip_probs(b, 1, 0)
                flip_probs(b, 1, 1)
                out0_flip(a)
                flip_probs(b, 1, 2)
                flip_probs(b, 1, 3)
                out0(a)
                for j in range(QUADS):
                    mix1(b, j)
                out1_flip(b, 0)
                out1_flip(b, 1)
                h1_flip(a)
                out1(b)
                route(a)
                experts(a, 0)
                places(a)
                experts(a, 1)
                if not later(b):
                    sum_sizes()
                if more:
                    embed(a + 1)
                xq_flip(b)
                experts(a, 2)
                for u in range(4):
                    gate_up(b, u)
                experts(a, 3)
                if more:
                    project0(a + 1)
                hq_flip(b, 0)
                hq_flip(b, 1)
                down(b)

            pe.wait_ge(w_in["const"], 64)
            pe.wait_ge(w_in["tok"], 16)
            stage_a(0)
            pe.wait_ge(w_in["qk1"], 16)
            pe.wait_ge(w_in["v1"], 16)
            pe.wait_ge(w_in["o1"], 16)
            both(1, 0)
            with pe.Fori(2, NG - 1) as g:
                both(g, g - 1)
            both(NG - 1, NG - 2, more=False)
            stage_b(NG - 1)

        @block.scalar
        def _(act):
            def copy(o, i, scale=1.0):
                return nc.scalar.activation(o, i, ACT.Copy, scale=scale)

            def rows(ps, n):
                return ps[:, 0:n * GT].rearrange("p (k t) -> p k t", k=n)

            def keep_qk0(g):
                act.wait_ge(full["qk0"], g + 1)
                ps = rows(bank_of("A", "qk0"), 4)
                for par in range(2):
                    nc.scalar.activation(q0[:, par, :, :], ps[:, 0:2, :], ACT.Copy, scale=parity[:, par:par + 1])
                copy(k0[:, :, :], ps[:, 2:4, :]).then_inc(drained["qk0"], 1)
                act.wait_ge(full["v0"], g + 1)
                ps = bank_of("A", "v0")
                copy(v0[:, :, 0:D0], ps[0:GT, 0:D].rearrange("p (h d) -> p h d", h=H)).then_inc(drained["v0"], 1)

            def exponentials(g, layer, j):
                act.wait_ge(shifted[layer], QUADS * g + j + 1)
                p = (p0, p1)[layer][:, 4 * j:4 * j + 4, :]
                nc.scalar.activation(p, p, ACT.Exp).then_inc(probs[layer], 1)

            def keep_flipped(g, layer, j):
                act.wait_ge(full[f"p{layer}"], QUADS * g + j + 1)
                ps = bank_of("AB"[layer], f"p{layer}", j)
                copy((p0t, p1t)[layer][:, 4 * j:4 * j + 4, :], rows(ps, 4)[0:GT]).then_inc(drained[f"p{layer}"], 1)

            def keep_rows(g, stage, kind, dst, n, u=0, per=1):
                act.wait_ge(full[kind], per * g + u + 1)
                copy(dst, rows(bank_of(stage, kind, u), n)).then_inc(drained[kind], 1)

            def keep_qk1(g, u):
                act.wait_ge(full["qk1"], 4 * g + u + 1)
                ps = rows(bank_of("B", "qk1", u), 4)
                dst = (q1, k1)[u % 2][:, 4 * (u // 2):4 * (u // 2) + 4, :]
                copy(dst, ps, D1 ** -0.5 if u % 2 == 0 else 1.0).then_inc(drained["qk1"], 1)

            def keep_v1(g, u):
                act.wait_ge(full["v1"], 2 * g + u + 1)
                ps = bank_of("B", "v1", u)
                copy(v1[:, 8 * u:8 * u + 8, 0:D1], ps[0:GT, :].rearrange("p (h d) -> p h d", h=8)).then_inc(drained["v1"], 1)

            def gap_exp(g):
                act.wait_ge(gap_ready, g + 1)
                nc.scalar.activation(egap[:, :], gap[:, :], ACT.Exp).then_inc(egap_ready, 1)

            def round_x(g):
                act.wait_ge(xscale_ready, g + 1)
                nc.scalar.activation(xr[:, :], h3[:, :], ACT.Identity, scale=xscale[:, :], bias=magic_t[0:GT, :]).then_inc(xr_ready, 1)

            def keep_xqt(g):
                act.wait_ge(full["xqt"], g + 1)
                ps = bank_of("B", "xqt")[:, :].bitcast(BF16)[:, 0:KD * 112].rearrange("p (k t) -> p k t", k=KD)
                copy(xqt[:, :, :], ps[:, :, 0:GT]).then_inc(drained["xqt"], 1)

            def relu_gate(g, half):
                act.wait_ge(full["gu"], 4 * g + 2 * half + 1)
                if later(g):
                    act.wait_ge(hid_ready, 2 * g)
                nc.scalar.activation(relu[:, half, :], bank_of("B", "gu", 2 * half)[0:GT, :], ACT.Relu).then_inc(relu_ready, 1)
                act.wait_ge(relu_ready, 2 * g + half + 1)
                nc.scalar.activation(relu[:, half, :], relu[:, half, :], ACT.Square).then_inc(relu2_ready, 1)

            def round_h(g, half):
                act.wait_ge(hscale_ready, 2 * g + 1)
                nc.scalar.activation(hidr[:, half * 512:half * 512 + 512], hid[:, half, :], ACT.Identity,
                                     scale=hscale[:, :], bias=magic_t[0:GT, :]).then_inc(hidr_ready, 1)

            def keep_hqt(g, u):
                act.wait_ge(full["hqt"], 2 * g + u + 1)
                ps = bank_of("B", "hqt", u)[:, :].bitcast(BF16)[:, 0:4 * 112].rearrange("p (k t) -> p k t", k=4)
                copy(hqt[:, 4 * u:4 * u + 4, :], ps[:, :, 0:GT]).then_inc(drained["hqt"], 1)

            def stage_a(g):
                keep_qk0(g)
                for j in range(QUADS):
                    exponentials(g, 0, j)
                for j in range(QUADS):
                    keep_flipped(g, 0, j)
                keep_rows(g, "A", "t0", o0t[:, :, :], KD)
                keep_rows(g, "A", "h1t", h1t[:, :, :], KD)
                gap_exp(g)
                keep_qk0(g + 1)

            def stage_b(g):
                keep_rows(g, "B", "h2t", h2t[:, :, :], KD)
                for u in range(4):
                    keep_qk1(g, u)
                for u in range(2):
                    keep_v1(g, u)
                for j in range(QUADS):
                    exponentials(g, 1, j)
                for j in range(QUADS):
                    keep_flipped(g, 1, j)
                for u in range(2):
                    keep_rows(g, "B", "t1", o1t[:, 4 * u:4 * u + 4, :], 4, u, 2)
                round_x(g)
                keep_xqt(g)
                relu_gate(g, 0)
                relu_gate(g, 1)
                round_h(g, 0)
                round_h(g, 1)
                keep_hqt(g, 0)
                keep_hqt(g, 1)

            def both(a, b, more=True):
                keep_rows(b, "B", "h2t", h2t[:, :, :], KD)
                exponentials(a, 0, 0)
                keep_qk1(b, 0)
                exponentials(a, 0, 1)
                keep_qk1(b, 1)
                exponentials(a, 0, 2)
                keep_qk1(b, 2)
                exponentials(a, 0, 3)
                keep_qk1(b, 3)
                keep_flipped(a, 0, 0)
                keep_v1(b, 0)
                keep_flipped(a, 0, 1)
                keep_v1(b, 1)
                for j in range(QUADS):
                    if j < 2:
                        keep_flipped(a, 0, 2 + j)
                    exponentials(b, 1, j)
                keep_flipped(b, 1, 0)
                keep_flipped(b, 1, 1)
                keep_rows(a, "A", "t0", o0t[:, :, :], KD)
                keep_flipped(b, 1, 2)
                keep_flipped(b, 1, 3)
                keep_rows(b, "B", "t1", o1t[:, 0:4, :], 4, 0, 2)
                keep_rows(b, "B", "t1", o1t[:, 4:8, :], 4, 1, 2)
                keep_rows(a, "A", "h1t", h1t[:, :, :], KD)
                gap_exp(a)
                round_x(b)
                keep_xqt(b)
                relu_gate(b, 0)
                relu_gate(b, 1)
                round_h(b, 0)
                round_h(b, 1)
                if more:
                    keep_qk0(a + 1)
                keep_hqt(b, 0)
                keep_hqt(b, 1)

            act.wait_ge(w_in["const"], 64)
            act.wait_ge(tables_ready, 6)
            stage_a(0)
            both(1, 0)
            with act.Fori(2, NG - 1) as g:
                both(g, g - 1)
            both(NG - 1, NG - 2, more=False)
            stage_b(NG - 1)

        @block.vector
        def _(dve):
            def keep_h0t(g):
                dve.wait_ge(full["tok"], g + 1)
                ps = bank_of("A", "tok")[:, 0:KD * GT].rearrange("p (k i s) -> p k i s", k=KD, i=IMG)
                for k in range(KD):
                    last = nc.vector.tensor_tensor(h0t[:, k, :].rearrange("p (i s) -> p i s", i=IMG), ps[:, k],
                                                   pos_t[:, k:k + 1, :].to_broadcast([128, IMG, S]), ALU.add)
                last.then_inc(drained["tok"], 1)

            def shift(g, layer, j):
                dve.wait_ge(full[f"s{layer}"], QUADS * g + j + 1)
                ps = bank_of("AB"[layer], f"s{layer}", j)[0:GT, 0:4 * GT].rearrange("p (h t) -> p h t", h=4)
                nm = (nmax0, nmax1)[layer][:, 4 * j:4 * j + 4]
                nc.vector.tensor_reduce(nm, ps, AX.X, ALU.max, negate=True).then_inc(nmax_ready[layer], 1)
                dve.wait_ge(nmax_ready[layer], QUADS * g + j + 1)
                nc.vector.tensor_tensor(
                    (p0, p1)[layer][:, 4 * j:4 * j + 4, :], ps, nm.unsqueeze(2).to_broadcast([GT, 4, GT]), ALU.add
                ).then_inc(shifted[layer], 1)
                dve.wait_ge(shifted[layer], QUADS * g + j + 1)

            def normalise(g, layer, j, heads, width, dst):
                kind = f"o{layer}"
                per = FILLS[kind]
                dve.wait_ge(full[kind], per * g + j + 1)
                ps = bank_of("AB"[layer], kind, j)[0:GT, 0:heads * (width + 1)].rearrange("p (h d) -> p h d", h=heads)
                rs = (rsum0, rsum1)[layer][:, heads * j:heads * (j + 1)]
                nc.vector.reciprocal(rs, ps[:, :, width]).then_inc(rsum_ready[layer], 1)
                dve.wait_ge(rsum_ready[layer], per * g + j + 1)
                nc.vector.tensor_tensor(dst.rearrange("p (h d) -> p h d", h=heads), ps[:, :, 0:width],
                                        rs.unsqueeze(2).to_broadcast([GT, heads, width]), ALU.mult).then_inc(drained[kind], 1)

            def variance(g, i, src):
                nc.vector.bn_stats(stats[:, i, :], src).then_inc(ln_stats[i], 1)
                dve.wait_ge(ln_stats[i], g + 1)
                dve.nop(nofuse=True)
                nc.vector.bn_aggr(mv[:, i, :], stats[:, i, :]).then_inc(ln_var[i], 1)

            def standardise(g, i, dst, src):
                dve.wait_ge(ln_var[i], g + 1)
                dve.wait_ge(ln_rstd[i], g + 1)
                return nc.vector.tensor_scalar(dst, src, mv[:, i, 0:1], rstd[:, i:i + 1], ALU.subtract, ALU.mult)

            def norm0_front(g):
                dve.wait_ge(full["y0"], g + 1)
                variance(g, 0, bank_of("A", "y0")[0:GT, 0:D])

            def norm0_back(g):
                standardise(g, 0, h1[:, :], bank_of("A", "y0")[0:GT, 0:D]).then_inc(h1_ready, 1)

            def choose(g):
                dve.wait_ge(full["logit"], g + 1)
                nc.vector.tensor_copy(logit[:, :], bank_of("A", "logit")[0:GT, 0:E]).then_inc(drained["logit"], 1)
                dve.wait_ge(drained["logit"], g + 1)
                dve.nop(nofuse=True)
                nc.vector.max(top[:, :], logit[:, :]).then_inc(top_ready, 1)
                dve.wait_ge(top_ready, g + 1)
                dve.nop(nofuse=True)
                nc.vector.max_index(top_at[:, :], top[:, :], logit[:, :]).then_inc(at_ready, 1)
                nc.vector.tensor_tensor(gap[:, :], top[:, 1:2], top[:, 0:1], ALU.subtract).then_inc(gap_ready, 1)
                dve.wait_ge(at_ready, g + 1)
                nc.vector.tensor_copy(top_atf[:, :], top_at[:, 0:2]).then_inc(atf_ready, 1)
                dve.wait_ge(atf_ready, g + 1)
                nc.vector.tensor_scalar(first[:, :], iota, top_atf[:, 0:1], None, ALU.is_equal).then_inc(onehot_ready, 1)
                nc.vector.tensor_scalar(second[:, :], iota, top_atf[:, 1:2], None, ALU.is_equal).then_inc(onehot_ready, 1)
                dve.wait_ge(onehot_ready, 2 * g + 2)
                nc.vector.tensor_tensor(chosen[:, :], first[:, :], second[:, :], ALU.add).then_inc(chosen_ready, 1)

            def gate_weights(g):
                dve.wait_ge(egap_ready, g + 1)
                nc.vector.tensor_scalar(esum[:, :], egap[:, :], 1.0, None, ALU.add).then_inc(esum_ready, 1)
                dve.wait_ge(esum_ready, g + 1)
                nc.vector.reciprocal(share[:, 0:1], esum[:, :]).then_inc(share1_ready, 1)
                dve.wait_ge(share1_ready, g + 1)
                nc.vector.tensor_tensor(share[:, 1:2], egap[:, :], share[:, 0:1], ALU.mult).then_inc(share2_ready, 1)
                nc.vector.tensor_scalar(gate1[:, :], first[:, :], share[:, 0:1], None, ALU.mult).then_inc(gate1_ready, 1)
                dve.wait_ge(share2_ready, g + 1)
                dve.wait_ge(gate1_ready, g + 1)
                nc.vector.scalar_tensor_tensor(gate2[:, :], second[:, :], share[:, 1:2], gate1[:, :], ALU.mult, ALU.add).then_inc(gate2_ready, 1)
                dve.wait_ge(full["place"], g + 1)
                dve.wait_ge(gate2_ready, g + 1)
                nc.vector.scalar_tensor_tensor(gates[:, :], bank_of("A", "place")[0:GT, 0:E], float(CAP), gate2[:, :],
                                               ALU.is_lt, ALU.mult).then_inc(drained["place"], 1)

            def add_experts(g, u):
                dve.wait_ge(full["moe"], 4 * g + u + 1)
                if u == 0:
                    dve.wait_ge(drained["place"], g + 1)
                ps = bank_of("A", "moe", u)
                for i in range(2):
                    e = 2 * u + i
                    if e > 0:
                        dve.wait_ge(drained["moe"], E * g + e)
                    nc.vector.scalar_tensor_tensor(acc[:, :], ps[0:GT, i * D:(i + 1) * D], gates[:, e:e + 1],
                                                   (h1 if e == 0 else acc)[:, :], ALU.mult, ALU.add).then_inc(drained["moe"], 1)

            def norm1_front(g):
                dve.wait_ge(drained["moe"], E * g + E)
                variance(g, 1, acc[:, :])

            def norm1_back(g):
                standardise(g, 1, h2[:, :], acc[:, :]).then_inc(h2_ready, 1)

            def norm2_front(g):
                dve.wait_ge(full["y1"], g + 1)
                nc.vector.tensor_tensor(z1[:, :], bank_of("B", "y1")[0:GT, 0:D], h2[:, :], ALU.add).then_inc(drained["y1"], 1)
                dve.wait_ge(drained["y1"], g + 1)
                variance(g, 2, z1[:, :])

            def norm2_back(g):
                standardise(g, 2, h3[:, :], z1[:, :]).then_inc(h3_ready, 1)

            def quantise_x(g):
                dve.wait_ge(h3_ready, g + 1)
                nc.vector.tensor_reduce(xmax[:, :], h3[:, :], AX.X, ALU.max, apply_absolute_value=True).then_inc(xmax_ready, 1)
                dve.wait_ge(xmax_ready, g + 1)
                nc.vector.tensor_scalar(xtop[:, :], xmax[:, :], EPS, None, ALU.max).then_inc(xtop_ready, 1)
                dve.wait_ge(xtop_ready, g + 1)
                nc.vector.reciprocal(xinv[:, :], xtop[:, :]).then_inc(xinv_ready, 1)
                dve.wait_ge(xinv_ready, g + 1)
                nc.vector.tensor_scalar(xscale[:, :], xinv[:, :], 127.0, None, ALU.mult).then_inc(xscale_ready, 1)
                nc.vector.tensor_scalar(xstep[:, :], xtop[:, :], 1.0 / 127.0, None, ALU.mult).then_inc(xstep2_ready, 1)
                dve.wait_ge(xstep2_ready, 2 * g + 1)
                nc.vector.tensor_tensor(xstep2[:, :], xstep[:, :], xstep[:, :], ALU.mult).then_inc(xstep2_ready, 1)
                dve.wait_ge(xstep2_ready, 2 * g + 2)
                nc.vector.scalar_tensor_tensor(hstep[:, :], xstep2[:, :], xstep[:, :], gu_size[0:GT, :], ALU.mult, ALU.mult).then_inc(hstep_ready, 1)
                dve.wait_ge(xr_ready, g + 1)
                nc.vector.tensor_scalar(xq[:, :], xr[:, :], ROUND, 127.0, ALU.subtract, ALU.min).then_inc(xq_ready, 1)

            def hidden(g, half):
                dve.wait_ge(full["gu"], 4 * g + 2 * half + 2)
                dve.wait_ge(relu2_ready, 2 * g + half + 1)
                nc.vector.tensor_tensor(hid[:, half, :], relu[:, half, :], bank_of("B", "gu", 2 * half + 1)[0:GT, :], ALU.mult).then_inc(hid_ready, 1)
                dve.wait_ge(hid_ready, 2 * g + half + 1)
                nc.vector.tensor_reduce(hmax[:, half:half + 1], hid[:, half, :], AX.X, ALU.max, apply_absolute_value=True).then_inc(hmax_ready, 1)

            def scale_h(g):
                dve.wait_ge(hmax_ready, 2 * g + 2)
                dve.wait_ge(hstep_ready, g + 1)
                nc.vector.tensor_scalar(htop[:, :], hmax[:, 0:1], hmax[:, 1:2], hstep[:, :], ALU.max, ALU.mult).then_inc(htop_ready, 1)
                dve.wait_ge(htop_ready, 2 * g + 1)
                nc.vector.tensor_scalar(htop[:, :], htop[:, :], EPS, None, ALU.max).then_inc(htop_ready, 1)
                dve.wait_ge(htop_ready, 2 * g + 2)
                nc.vector.reciprocal(hinv[:, :], htop[:, :]).then_inc(hinv_ready, 1)
                dve.wait_ge(hinv_ready, g + 1)
                nc.vector.tensor_scalar(hscale[:, :], hinv[:, :], hstep[:, :], 127.0, ALU.mult, ALU.mult).then_inc(hscale_ready, 1)
                nc.vector.tensor_scalar(ystep[:, :], htop[:, :], wmean[0:GT, 2:3], 1.0 / 127.0, ALU.mult, ALU.mult).then_inc(hscale_ready, 1)

            def quantise_h(g, half):
                c = slice(half * 512, half * 512 + 512)
                dve.wait_ge(hidr_ready, 2 * g + half + 1)
                nc.vector.tensor_scalar(hq[:, c], hidr[:, c], ROUND, 127.0, ALU.subtract, ALU.min).then_inc(hq_ready, 1)

            def norm3(g):
                dve.wait_ge(full["down"], g + 1)
                dve.wait_ge(hscale_ready, 2 * g + 2)
                nc.vector.scalar_tensor_tensor(z2[:, :], bank_of("B", "down")[0:GT, 0:D], ystep[:, :], h3[:, :],
                                               ALU.mult, ALU.add).then_inc(drained["down"], 1)
                dve.wait_ge(drained["down"], g + 1)
                variance(g, 3, z2[:, :])
                if later(g):
                    dve.wait_ge(out_done, 16 * g)
                standardise(g, 3, res[:, :], z2[:, :]).then_inc(out_ready, 1)

            def stage_a(g):
                keep_h0t(g)
                for j in range(QUADS):
                    shift(g, 0, j)
                normalise(g, 0, 0, H, D0, o0[:, :])
                norm0_front(g)
                norm0_back(g)
                choose(g)
                gate_weights(g)
                add_experts(g, 0)
                keep_h0t(g + 1)
                for u in range(1, 4):
                    add_experts(g, u)
                norm1_front(g)
                norm1_back(g)

            def stage_b(g):
                for j in range(QUADS):
                    shift(g, 1, j)
                for j in range(QUADS):
                    normalise(g, 1, j, 4, D1, o1[:, 256 * j:256 * j + 256])
                norm2_front(g)
                norm2_back(g)
                quantise_x(g)
                hidden(g, 0)
                hidden(g, 1)
                scale_h(g)
                quantise_h(g, 0)
                quantise_h(g, 1)
                norm3(g)

            def both(a, b, more=True):
                for j in range(QUADS):
                    shift(a, 0, j)
                for j in range(QUADS):
                    shift(b, 1, j)
                normalise(a, 0, 0, H, D0, o0[:, :])
                norm0_front(a)
                for j in range(2):
                    normalise(b, 1, j, 4, D1, o1[:, 256 * j:256 * j + 256])
                norm0_back(a)
                for j in range(2, 4):
                    normalise(b, 1, j, 4, D1, o1[:, 256 * j:256 * j + 256])
                norm2_front(b)
                choose(a)
                norm2_back(b)
                if not later(b):
                    ternary_sizes()
                quantise_x(b)
                gate_weights(a)
                add_experts(a, 0)
                if more:
                    keep_h0t(a + 1)
                add_experts(a, 1)
                add_experts(a, 2)
                hidden(b, 0)
                hidden(b, 1)
                scale_h(b)
                add_experts(a, 3)
                quantise_h(b, 0)
                quantise_h(b, 1)
                norm1_front(a)
                norm1_back(a)
                norm3(b)

            def ternary_sizes():
                dve.wait_ge(w_in["ff"], 48)
                for i in range(3):
                    nc.vector.tensor_reduce(wabs[:, i:i + 1], wff[:, i, :], AX.X, ALU.add, apply_absolute_value=True).then_inc(wabs_ready, 1)
                dve.wait_ge(wsum_full, 1)
                nc.vector.tensor_scalar(wmean[:, :], bank_of("B", "xqt")[:, 0:3], 1.0 / (D * FF), EPS, ALU.mult, ALU.max).then_inc(wmean_ready, 1)
                dve.wait_ge(wmean_ready, 1)
                nc.vector.reciprocal(winv[:, :], wmean[:, :]).then_inc(winv_ready, 1)
                nc.vector.tensor_tensor(gu_size[:, :], wmean[:, 0:1], wmean[:, 0:1], ALU.mult).then_inc(gu_sq, 1)
                dve.wait_ge(gu_sq, 1)
                nc.vector.tensor_tensor(gu_size[:, :], gu_size[:, :], wmean[:, 1:2], ALU.mult).then_inc(gu_size_ready, 1)
                dve.wait_ge(winv_ready, 1)
                for i in range(3):
                    nc.vector.tensor_scalar(wff[:, i, :], wff[:, i, :], winv[:, i:i + 1], 1.0, ALU.mult, ALU.min).then_inc(wclip, 1)
                    dve.wait_ge(wclip, i + 1)
                    nc.vector.tensor_scalar(wff[:, i, :], wff[:, i, :], -1.0, ROUND, ALU.max, ALU.add).then_inc(wround, 1)
                    dve.wait_ge(wround, i + 1)
                    nc.vector.tensor_scalar(wq[:, i, :], wff[:, i, :], ROUND, None, ALU.subtract).then_inc(wq_ready, 1)
                dve.wait_ge(gu_size_ready, 1)

            dve.wait_ge(w_in["const"], 64)
            for k in range(KD):
                nc.vector.tensor_scalar(pos_t[:, k, 1:S], pos_t[:, k, 1:S], tokb_t[:, k:k + 1], None, ALU.add).then_inc(posb_sum, 1)
                nc.vector.tensor_scalar(pos_t[:, k, 0:1], pos_t[:, k, 0:1], cls_t[:, k:k + 1], None, ALU.add).then_inc(posb_sum, 1)
            nc.vector.tensor_copy(ident_b[:, :], ident).then_inc(tables_ready, 1)
            nc.vector.tensor_copy(mask_b[:, :, :], mask_f.unsqueeze(1).to_broadcast([GT, 4, GT])).then_inc(tables_ready, 1)
            nc.vector.tensor_copy(before_b[:, :], before_f).then_inc(tables_ready, 1)
            nc.vector.memset(eps_t[:, :], EPS).then_inc(tables_ready, 1)
            nc.vector.memset(magic_t[:, :], ROUND).then_inc(tables_ready, 1)
            nc.vector.memset(mhalf[:, :], -0.5).then_inc(tables_ready, 1)
            nc.vector.memset(v0[:, :, D0:D0 + 1], 1.0)
            nc.vector.memset(v1[:, :, D1:D1 + 1], 1.0)
            nc.vector.memset(ones[:, :], 1.0)
            dve.wait_ge(posb_sum, 2 * KD)
            stage_a(0)
            both(1, 0)
            with dve.Fori(2, NG - 1) as g:
                both(g, g - 1)
            both(NG - 1, NG - 2, more=False)
            stage_b(NG - 1)

        @block.gpsimd
        def _(pool):
            def deviation(g, i):
                pool.wait_ge(ln_var[i], g + 1)
                pool.nop(nofuse=True)
                nc.gpsimd.tensor_scalar(lnv[:, i:i + 1], mv[:, i, 1:2], EPS, None, ALU.add).then_inc(ln_log[i], 1)
                pool.wait_ge(ln_log[i], g + 1)
                nc.gpsimd.tensor_tensor(rstd[:, i:i + 1], lnv[:, i:i + 1], mhalf[0:GT, :], ALU.pow).then_inc(ln_rstd[i], 1)

            pool.wait_ge(tables_ready, 6)
            deviation(0, 0)
            deviation(0, 1)
            with pool.Fori(1, NG) as g:
                deviation(g, 0)
                deviation(g - 1, 2)
                deviation(g, 1)
                deviation(g - 1, 3)
            deviation(NG - 1, 2)
            deviation(NG - 1, 3)


_ORDER = ["xp", "consts", "pos", "cls", "tokb", "tokw", "qk0w", "v0w", "o0w", "wr", "we", "qk1w", "v1w", "o1w", "wg", "wu", "wd"]


def kernel(**inputs):
    import concourse.bacc as _bacc
    from concourse.bass_utils import run_bass_kernel_spmd as _run

    a = {k: np.asarray(v) for k, v in inputs.items()}

    def rows(w, k):
        return np.ascontiguousarray(w.reshape(k, 128, -1).transpose(1, 0, 2))

    patches = a["x"].reshape(B, CH, PER_SIDE, PATCH, PER_SIDE, PATCH).transpose(0, 2, 4, 1, 3, 5).reshape(B, S - 1, PD)
    xs = np.zeros((NG * IMG, S, PD), patches.dtype)
    xs[:B, 1:] = patches
    xp = xs.reshape(NG, GT, KP, 128).transpose(0, 3, 2, 1)

    t = np.arange(GT)
    same = t[:, None] // S == t[None, :] // S
    consts = np.zeros((128, 128 + 2 * GT + 2 + E), np.float32)
    consts[:, 0:128] = np.eye(128)
    consts[:GT, 128:128 + GT] = np.where(same & (t[None, :] <= t[:, None]), 0.0, MASKED)
    consts[:GT, 128 + GT:128 + 2 * GT] = same & (t[:, None] < t[None, :])
    p = np.arange(128)
    for par in range(2):
        consts[:, 128 + 2 * GT + par] = np.where(p // D0 % 2 == par, D0 ** -0.5, 0.0)
    consts[:, 130 + 2 * GT:] = np.arange(E)

    heads0 = [4 * j + 2 * t_ + par for t_ in range(2) for j in range(4) for par in range(2)]
    cols0 = np.concatenate([np.arange(h * D0, (h + 1) * D0) for h in heads0])
    qk0 = np.concatenate([a["L0_attn_q_heads"].T[:, cols0], a["L0_attn_k_heads"].T[:, cols0]], 1)
    def pair(w, half):
        w = w.transpose(2, 0, 1)
        order = [8 * half + i + 4 * z for i in range(4) for z in range(2)]
        return w[:, order, :].reshape(D, -1)
    q, k = a["L1_attn_w_q"], a["L1_attn_w_k"]
    qk1 = np.concatenate([pair(q, 0), pair(k, 0), pair(q, 1), pair(k, 1)], 1)

    data = {
        "xp": xp, "consts": consts,
        "pos": a["L0_tok_pos_embedding"].reshape(S, KD, 128).transpose(2, 1, 0),
        "cls": a["L0_tok_cls_token"].reshape(KD, 128).T,
        "tokb": a["L0_tok_b"].reshape(KD, 128).T,
        "tokw": rows(a["L0_tok_W"].T, KP),
        "qk0w": rows(qk0, KD),
        "v0w": rows(a["L0_attn_v_heads"].T, KD),
        "o0w": rows(a["L0_attn_output_proj"].T, KD),
        "wr": rows(a["L0_ffn_Wr"].T, KD),
        "we": rows(a["L0_ffn_We"].transpose(1, 0, 2).reshape(D, E * D), KD),
        "qk1w": rows(qk1, KD),
        "v1w": rows(a["L1_attn_w_v"].transpose(2, 0, 1).reshape(D, W1), KD),
        "o1w": rows(a["L1_attn_w_o"], KO),
        "wg": rows(a["L1_ffn_w_gate"].T, KD).reshape(128, -1),
        "wu": rows(a["L1_ffn_w_up"].T, KD).reshape(128, -1),
        "wd": rows(a["L1_ffn_w_down"].T, KF).reshape(128, -1),
    }
    nc = _bacc.Bacc("TRN2", target_bir_lowering=False, num_devices=1)
    arrays, args = {}, []
    for name in _ORDER:
        v = np.ascontiguousarray(data[name])
        arrays[f"in_{name}"] = v
        args.append(nc.dram_tensor(f"in_{name}", v.shape, mybir.dt.from_np(v.dtype), kind="ExternalInput").ap())
    out = nc.dram_tensor("tokens_out", (NG, GT, D), F32, kind="ExternalOutput").ap()
    vit_tower(nc, *args, out)
    r = _run(nc, [arrays], core_ids=[0])
    return r.results[0]["tokens_out"].reshape(NG * IMG, S, D)[:B]
```

```python
from contextlib import ExitStack

import numpy as np
import concourse.bass as bass
from concourse import mybir

F32 = mybir.dt.float32
BF16 = mybir.dt.bfloat16
U32 = mybir.dt.uint32
ALU = mybir.AluOpType
ACT = mybir.ActivationFunctionType
AX = mybir.AxisListType

B, SIDE, PATCH, CH = 32, 96, 16, 3
PER_SIDE = SIDE // PATCH
S = PER_SIDE * PER_SIDE + 1
D = 256
PD = CH * PATCH * PATCH
IMG = 3
GT = IMG * S
NG = -(-B // IMG)
KP = PD // 128
KD = D // 128
H = 16
QUADS = 4
D0 = D // H
D1 = 64
W1 = H * D1
KO = W1 // 128
E = 8
CAP = int(S * 2 / E * 1.5) + 1
FF = 1024
KF = FF // 128
EPS = 1e-5
MASKED = -1e30
ROUND = 1.5 * 2.0 ** 23


def fillings(kind, numbers, ahead=0):
    return [(kind, u, ahead) for u in numbers]


A_SLOTS = (fillings("s0", (2, 3)) + fillings("p0", range(QUADS)) + fillings("o0", (0,)) + fillings("t0", (0,))
           + fillings("y0", (0,)) + fillings("h1t", (0,)) + fillings("tok", (0,), 1) + fillings("logit", (0,))
           + fillings("moe", (0,)) + fillings("place", (0,)) + fillings("moe", (1, 2, 3)) + fillings("qk0", (0,), 1)
           + fillings("v0", (0,), 1) + fillings("s0", (0, 1), 1))
B_SLOTS = (fillings("qk1", (3,)) + fillings("v1", (0,)) + fillings("s1", range(QUADS)) + fillings("v1", (1,))
           + fillings("p1", range(QUADS)) + fillings("o1", (0, 1)) + fillings("t1", (0,))
           + fillings("o1", (2, 3)) + fillings("y1", (0,)) + fillings("t1", (1,)) + fillings("xqt", (0,)) + fillings("gu", range(4)) + fillings("h2t", (0,), 1)
           + fillings("qk1", (0, 1), 1) + fillings("hqt", range(2)) + fillings("qk1", (2,), 1) + fillings("down", (0,)))
A_BANKS, B_BANKS = 3, 5
assert len(A_SLOTS) % A_BANKS == 0 and len(B_SLOTS) % B_BANKS == 0
KINDS = list(dict.fromkeys(k for k, _, _ in A_SLOTS + B_SLOTS))
FILLS = {k: [x for x, _, _ in A_SLOTS + B_SLOTS].count(k) for k in KINDS}


def vit_tower(nc, xp, consts, pos, cls, tokb, tokw, qk0w, v0w, o0w, wr, we, qk1w, v1w, o1w, wg, wu, wd, out):
    ctx = ExitStack()
    with ctx:
        def sb(name, shape, dt=F32):
            return ctx.enter_context(nc.sbuf_tensor(name, shape, dt))

        def sem(name):
            return ctx.enter_context(nc.semaphore(name))

        cst = sb("cst", [128, 128 + 2 * GT + 2 + E])
        ident = cst[:, 0:128]
        mask_f = cst[0:GT, 128:128 + GT]
        before_f = cst[0:GT, 128 + GT:128 + 2 * GT]
        parity = cst[:, 128 + 2 * GT:130 + 2 * GT]
        iota = cst[0:GT, 130 + 2 * GT:130 + 2 * GT + E]
        ident_b = sb("ident_b", [128, 128], BF16)
        mask_b = sb("mask_b", [GT, 4, GT], BF16)
        before_b = sb("before_b", [GT, GT], BF16)
        ones = sb("ones", [128, 128])
        eps_t = sb("eps_t", [128, 1])
        mhalf = sb("mhalf", [128, 1])
        magic_t = sb("magic_t", [128, 1])
        pos_t = sb("pos_t", [128, KD, S])
        cls_t = sb("cls_t", [128, KD])
        tokb_t = sb("tokb_t", [128, KD])
        tokw_t = sb("tokw_t", [128, KP, D])
        qk0w_t = sb("qk0w_t", [128, KD, 2 * D])
        v0w_t = sb("v0w_t", [128, KD, D])
        o0w_t = sb("o0w_t", [128, KD, D])
        wr_t = sb("wr_t", [128, KD, E])
        we_t = sb("we_t", [128, KD, E * D])
        qk1w_t = sb("qk1w_t", [128, KD, 2 * W1])
        v1w_t = sb("v1w_t", [128, KD, W1])
        o1w_t = sb("o1w_t", [128, KO, D])
        wff = sb("wff", [128, 3, 2048])
        wq = sb("wq", [128, 3, 2048], BF16)
        gate_q = wq[:, 0, :].rearrange("p (k n) -> p k n", k=KD)
        up_q = wq[:, 1, :].rearrange("p (k n) -> p k n", k=KD)
        down_q = wq[:, 2, :].rearrange("p (k n) -> p k n", k=KF)
        wabs = sb("wabs", [128, 3])
        wmean = sb("wmean", [128, 3])
        winv = sb("winv", [128, 3])
        gu_sq = sb("gu_sq", [128, 1])
        gu_size = sb("gu_size", [128, 1])

        x_in = sb("x_in", [128, KP, GT])
        h0t = sb("h0t", [128, KD, GT])
        q0 = sb("q0", [128, 2, KD, GT])
        k0 = sb("k0", [128, KD, GT])
        v0 = sb("v0", [GT, H, D0 + 1])
        nmax0 = sb("nmax0", [GT, H])
        p0 = sb("p0", [GT, H, GT])
        p0t = sb("p0t", [GT, H, GT])
        rsum0 = sb("rsum0", [GT, H])
        o0 = sb("o0", [GT, D])
        o0t = sb("o0t", [128, KD, GT])
        h1 = sb("h1", [GT, D])
        h1t = sb("h1t", [128, KD, GT])
        logit = sb("logit", [GT, E])
        top = sb("top", [GT, 8])
        top_at = sb("top_at", [GT, 8], U32)
        top_atf = sb("top_atf", [GT, 2])
        first = sb("first", [GT, E])
        second = sb("second", [GT, E])
        chosen = sb("chosen", [GT, E], BF16)
        gap = sb("gap", [GT, 1])
        egap = sb("egap", [GT, 1])
        esum = sb("esum", [GT, 1])
        share = sb("share", [GT, 1])
        gate1 = sb("gate1", [GT, E])
        gate2 = sb("gate2", [GT, E])
        gates = sb("gates", [GT, E])
        acc = sb("acc", [GT, D])
        h2 = sb("h2", [GT, D])
        h2t = sb("h2t", [128, KD, GT])
        q1 = sb("q1", [128, 8, GT])
        k1 = sb("k1", [128, 8, GT])
        v1 = sb("v1", [GT, H, D1 + 1])
        nmax1 = sb("nmax1", [GT, H])
        p1 = sb("p1", [GT, H, GT])
        p1t = sb("p1t", [GT, H, GT])
        rsum1 = sb("rsum1", [GT, H])
        o1 = sb("o1", [GT, W1])
        o1t = sb("o1t", [128, KO, GT])
        z1 = sb("z1", [GT, D])
        h3 = sb("h3", [GT, D])
        xmax = sb("xmax", [GT, 1])
        hleast = sb("hleast", [GT, 1])
        hstep127 = sb("hstep127", [GT, 1])
        xscale = sb("xscale", [GT, 1])
        xstep = sb("xstep", [GT, 1])
        xstep2 = sb("xstep2", [GT, 1])
        hstep = sb("hstep", [GT, 1])
        xr = sb("xr", [GT, D])
        xq = sb("xq", [GT, D], BF16)
        xqt = sb("xqt", [128, KD, GT], BF16)
        relu = sb("relu", [GT, 2, 512])
        hid = sb("hid", [GT, 2, 512])
        hidr = sb("hidr", [GT, FF])
        hmax = sb("hmax", [GT, 2])
        hmax0 = sb("hmax0", [GT, 1])
        hsize = sb("hsize", [GT, 1])
        hscale = sb("hscale", [GT, 1])
        ystep = sb("ystep", [GT, 1])
        hq = sb("hq", [GT, FF], BF16)
        hqt = sb("hqt", [128, KF, GT], BF16)
        z2 = sb("z2", [GT, D])
        res = sb("res", [GT, D])
        stats = sb("stats", [GT, 4, 6])
        mv = sb("mv", [GT, 4, 2])
        lnv = sb("lnv", [GT, 4])
        rstd = sb("rstd", [GT, 4])

        banks = [ctx.enter_context(nc.psum_tensor(f"bank{i}", [128, 512], F32)) for i in range(8)]

        full = {k: sem("full_" + k) for k in KINDS}
        drained = {k: sem("drained_" + k) for k in KINDS if k not in ("s0", "s1", "y0", "gu")}
        w_in = {k: sem("in_" + k) for k in
                ["const", "tok", "l0", "moe", "qk1", "v1", "o1", "ff"]}
        x_ready = sem("x_ready")
        out_done = sem("out_done")
        posb_sum = sem("posb_sum")
        tables_ready = sem("tables_ready")
        wabs_ready, wmean_ready = sem("wabs_ready"), sem("wmean_ready")
        winv_ready, gu_sq_ready, gu_size_ready = sem("winv_ready"), sem("gu_sq_ready"), sem("gu_size_ready")
        wclip, wround, wq_ready = sem("wclip"), sem("wround"), sem("wq_ready")
        wsum_full = sem("wsum_full")
        nmax_ready = [sem("nmax0_ready"), sem("nmax1_ready")]
        shifted = [sem("shifted0"), sem("shifted1")]
        probs = [sem("probs0"), sem("probs1")]
        rsum_ready = [sem("rsum0_ready"), sem("rsum1_ready")]
        ln_stats = [sem(f"ln_stats{i}") for i in range(4)]
        ln_var = [sem(f"ln_var{i}") for i in range(4)]
        ln_log = [sem(f"ln_log{i}") for i in range(4)]
        ln_rstd = [sem(f"ln_rstd{i}") for i in range(4)]
        h1_ready, h2_ready, h3_ready, out_ready = sem("h1_ready"), sem("h2_ready"), sem("h3_ready"), sem("out_ready")
        z1_ready, z2_ready = sem("z1_ready"), sem("z2_ready")
        top_ready, at_ready, atf_ready = sem("top_ready"), sem("at_ready"), sem("atf_ready")
        onehot_ready, chosen_ready, gap_ready, egap_ready = sem("onehot_ready"), sem("chosen_ready"), sem("gap_ready"), sem("egap_ready")
        esum_ready, share_ready = sem("esum_ready"), sem("share_ready")
        gate1_ready, gate2_ready = sem("gate1_ready"), sem("gate2_ready")
        xmax_ready, xstep_ready, xscale_ready = sem("xmax_ready"), sem("xstep_ready"), sem("xscale_ready")
        hstep127_ready, hleast_ready = sem("hstep127_ready"), sem("hleast_ready")
        xstep2_ready, hstep_ready = sem("xstep2_ready"), sem("hstep_ready")
        xr_ready, xq_ready = sem("xr_ready"), sem("xq_ready")
        relu_ready, relu2_ready, hid_ready = sem("relu_ready"), sem("relu2_ready"), sem("hid_ready")
        hmax_ready, hmax0_ready, hsize_ready, hscale_ready = sem("hmax_ready"), sem("hmax0_ready"), sem("hsize_ready"), sem("hscale_ready")
        ystep_ready = sem("ystep_ready")
        hidr0_ready, hidr_ready, hq_ready = sem("hidr0_ready"), sem("hidr_ready"), sem("hq_ready")

        def bank_of(stage, kind, u=0):
            slots, n, base = (A_SLOTS, A_BANKS, 0) if stage == "A" else (B_SLOTS, B_BANKS, A_BANKS)
            return banks[base + [x[:2] for x in slots].index((kind, u)) % n]

        def drained_when(kind, u, g):
            if kind in ("s0", "s1"):
                return shifted[int(kind[1])], QUADS * g + u + 1
            if kind == "y0":
                return h1_ready, g + 1
            if kind == "moe":
                return drained["moe"], E * g + 2 * u + 2
            if kind == "gu":
                return (relu_ready, hid_ready)[u % 2], 2 * g + u // 2 + 1
            return drained[kind], FILLS[kind] * g + u + 1

        def claim(pe, stage, kind, u, g):
            slots, n = (A_SLOTS, A_BANKS) if stage == "A" else (B_SLOTS, B_BANKS)
            at = [x[:2] for x in slots].index((kind, u))
            turn = g - slots[at][2]
            while True:
                at -= n
                if at < 0:
                    at, turn = at + len(slots), turn - 1
                k, v, ahead = slots[at]
                if not isinstance(g, int):
                    pe.wait_ge(*drained_when(k, v, turn + ahead))
                elif turn + ahead >= NG:
                    continue
                elif turn + ahead >= 0:
                    pe.wait_ge(*drained_when(k, v, turn + ahead))
                return bank_of(stage, kind, u)

        def later(g):
            return not (isinstance(g, int) and g == 0)

        block = ctx.enter_context(nc.Block())

        @block.sync
        def _(sp):
            sp.dma_start(cst[:, :], consts).then_inc(w_in["const"], 16)
            sp.dma_start(pos_t[:, :, :], pos).then_inc(w_in["const"], 16)
            sp.dma_start(cls_t[:, :], cls).then_inc(w_in["const"], 16)
            sp.dma_start(tokb_t[:, :], tokb).then_inc(w_in["const"], 16)
            sp.dma_start(tokw_t[:, :, :], tokw).then_inc(w_in["tok"], 16)
            sp.dma_start(x_in[:, :, :], xp[0]).then_inc(x_ready, 16)
            sp.dma_start(qk0w_t[:, :, :], qk0w).then_inc(w_in["l0"], 16)
            sp.dma_start(v0w_t[:, :, :], v0w).then_inc(w_in["l0"], 16)
            sp.dma_start(o0w_t[:, :, :], o0w).then_inc(w_in["l0"], 16)
            sp.dma_start(wr_t[:, :, :], wr).then_inc(w_in["moe"], 16)
            sp.dma_start(we_t[:, :, :], we).then_inc(w_in["moe"], 16)
            sp.wait_ge(full["tok"], 1)
            sp.dma_start(x_in[:, :, :], xp[1]).then_inc(x_ready, 16)
            sp.dma_start(wff[:, 0, :], wg).then_inc(w_in["ff"], 16)
            sp.dma_start(wff[:, 1, :], wu).then_inc(w_in["ff"], 16)
            sp.dma_start(wff[:, 2, :], wd).then_inc(w_in["ff"], 16)
            sp.dma_start(qk1w_t[:, :, :], qk1w).then_inc(w_in["qk1"], 16)
            sp.dma_start(v1w_t[:, :, :], v1w).then_inc(w_in["v1"], 16)
            sp.dma_start(o1w_t[:, :, :], o1w).then_inc(w_in["o1"], 16)

            def store(g):
                sp.wait_ge(out_ready, g + 1)
                sp.dma_start(out[g], res[:, :]).then_inc(out_done, 16)

            with sp.Fori(1, NG - 1) as g:
                sp.wait_ge(full["tok"], g + 1)
                sp.dma_start(x_in[:, :, :], xp[g + 1]).then_inc(x_ready, 16)
                store(g - 1)
            store(NG - 2)
            store(NG - 1)
            sp.wait_ge(out_done, 16 * NG)

        @block.tensor
        def _(pe):
            def mm(o, l, r, first=True, last=True):
                return nc.tensor.matmul(o, l, r, start=first, stop=last)

            def embed(g, halves=(0, 1)):
                if halves[0] == 0:
                    claim(pe, "A", "tok", 0, g)
                    pe.wait_ge(x_ready, 16 * g + 16)
                ps = bank_of("A", "tok")
                for m in halves:
                    for k in range(KP):
                        last = mm(ps[:, m * GT:(m + 1) * GT], tokw_t[:, k, m * 128:(m + 1) * 128], x_in[:, k, :],
                                  k == 0, k == KP - 1)
                if halves[-1] == KD - 1:
                    last.then_inc(full["tok"], 1)

            def project0(g):
                ps = claim(pe, "A", "qk0", 0, g)
                pe.wait_ge(drained["tok"], g + 1)
                for m in range(4):
                    for k in range(KD):
                        last = mm(ps[:, m * GT:(m + 1) * GT], qk0w_t[:, k, m * 128:(m + 1) * 128], h0t[:, k, :],
                                  k == 0, k == KD - 1)
                last.then_inc(full["qk0"], 1)

            def values0(g):
                ps = claim(pe, "A", "v0", 0, g)
                for k in range(KD):
                    last = mm(ps[0:GT, 0:D], h0t[:, k, :], v0w_t[:, k, :], k == 0, k == KD - 1)
                last.then_inc(full["v0"], 1)

            def mask(ps):
                mm(ps[0:GT, 0:4 * GT], ident_b[0:GT, 0:GT], mask_b[:, :, :], True, False)

            def scores0(g, j):
                ps = claim(pe, "A", "s0", j, g)
                if j == 0:
                    pe.wait_ge(drained["qk0"], g + 1)
                mask(ps)
                for i in range(4):
                    r = slice(32 * j, 32 * j + 32)
                    last = mm(ps[0:GT, i * GT:(i + 1) * GT], q0[r, i % 2, i // 2, :], k0[r, i // 2, :], False, i == 3)
                last.then_inc(full["s0"], 1)

            def flip_probs(g, layer, j):
                ps = claim(pe, "AB"[layer], f"p{layer}", j, g)
                pe.wait_ge(probs[layer], QUADS * g + j + 1)
                src = (p0, p1)[layer]
                for i in range(4):
                    last = nc.tensor.transpose(ps[0:GT, i * GT:(i + 1) * GT], src[:, 4 * j + i, :], ident[0:GT, 0:GT])
                last.then_inc(full[f"p{layer}"], 1)

            def mix0(g, j):
                if j == 0:
                    claim(pe, "A", "o0", 0, g)
                    pe.wait_ge(drained["v0"], g + 1)
                ps = bank_of("A", "o0")
                pe.wait_ge(drained["p0"], QUADS * g + j + 1)
                for h in range(4 * j, 4 * j + 4):
                    last = mm(ps[0:GT, h * (D0 + 1):(h + 1) * (D0 + 1)], p0t[:, h, :], v0[:, h, :])
                if j == QUADS - 1:
                    last.then_inc(full["o0"], 1)

            def out0_flip(g):
                ps = claim(pe, "A", "t0", 0, g)
                pe.wait_ge(drained["o0"], g + 1)
                for k in range(KD):
                    last = nc.tensor.transpose(ps[:, k * GT:(k + 1) * GT], o0[:, k * 128:(k + 1) * 128], ident[0:GT, 0:GT])
                last.then_inc(full["t0"], 1)

            def out0(g):
                ps = claim(pe, "A", "y0", 0, g)
                pe.wait_ge(drained["t0"], g + 1)
                for k in range(KD):
                    mm(ps[0:GT, 0:D], o0t[:, k, :], o0w_t[:, k, :], k == 0, False)
                for k in range(KD):
                    last = mm(ps[0:GT, k * 128:(k + 1) * 128], h0t[:, k, :], ident, False, k == KD - 1)
                last.then_inc(full["y0"], 1)

            def h1_flip(g):
                ps = claim(pe, "A", "h1t", 0, g)
                pe.wait_ge(h1_ready, g + 1)
                for k in range(KD):
                    last = nc.tensor.transpose(ps[:, k * GT:(k + 1) * GT], h1[:, k * 128:(k + 1) * 128], ident[0:GT, 0:GT])
                last.then_inc(full["h1t"], 1)

            def route(g):
                ps = claim(pe, "A", "logit", 0, g)
                pe.wait_ge(drained["h1t"], g + 1)
                for k in range(KD):
                    last = mm(ps[0:GT, 0:E], h1t[:, k, :], wr_t[:, k, :], k == 0, k == KD - 1)
                last.then_inc(full["logit"], 1)

            def experts(g, u):
                ps = claim(pe, "A", "moe", u, g)
                for k in range(KD):
                    last = mm(ps[0:GT, :], h1t[:, k, :], we_t[:, k, u * 512:(u + 1) * 512], k == 0, k == KD - 1)
                last.then_inc(full["moe"], 1)

            def places(g):
                ps = claim(pe, "A", "place", 0, g)
                pe.wait_ge(chosen_ready, g + 1)
                mm(ps[0:GT, 0:E], before_b[:, :], chosen[:, :]).then_inc(full["place"], 1)

            def h2_flip(g):
                ps = claim(pe, "B", "h2t", 0, g)
                pe.wait_ge(h2_ready, g + 1)
                for k in range(KD):
                    last = nc.tensor.transpose(ps[:, k * GT:(k + 1) * GT], h2[:, k * 128:(k + 1) * 128], ident[0:GT, 0:GT])
                last.then_inc(full["h2t"], 1)

            def project1(g, u):
                ps = claim(pe, "B", "qk1", u, g)
                if u == 0:
                    pe.wait_ge(drained["h2t"], g + 1)
                for m in range(4):
                    for k in range(KD):
                        c = (4 * u + m) * 128
                        last = mm(ps[:, m * GT:(m + 1) * GT], qk1w_t[:, k, c:c + 128], h2t[:, k, :], k == 0, k == KD - 1)
                last.then_inc(full["qk1"], 1)

            def values1(g, u):
                ps = claim(pe, "B", "v1", u, g)
                for k in range(KD):
                    last = mm(ps[0:GT, :], h2t[:, k, :], v1w_t[:, k, u * 512:(u + 1) * 512], k == 0, k == KD - 1)
                last.then_inc(full["v1"], 1)

            def scores1(g, j):
                ps = claim(pe, "B", "s1", j, g)
                pe.wait_ge(drained["qk1"], 4 * g + 2 * (j // 2) + 2)
                mask(ps)
                r = slice(64 * (j % 2), 64 * (j % 2) + 64)
                for i in range(4):
                    t = 4 * (j // 2) + i
                    last = mm(ps[0:GT, i * GT:(i + 1) * GT], q1[r, t, :], k1[r, t, :], False, i == 3)
                last.then_inc(full["s1"], 1)

            def mix1(g, j):
                ps = claim(pe, "B", "o1", j, g)
                if j == 0:
                    pe.wait_ge(drained["v1"], 2 * g + 2)
                pe.wait_ge(drained["p1"], QUADS * g + j + 1)
                for i in range(4):
                    h = 4 * j + i
                    last = mm(ps[0:GT, i * (D1 + 1):(i + 1) * (D1 + 1)], p1t[:, h, :], v1[:, h, :])
                last.then_inc(full["o1"], 1)

            def out1_flip(g, u):
                ps = claim(pe, "B", "t1", u, g)
                pe.wait_ge(drained["o1"], QUADS * g + 2 * u + 2)
                for i in range(4):
                    c = (4 * u + i) * 128
                    last = nc.tensor.transpose(ps[:, i * GT:(i + 1) * GT], o1[:, c:c + 128], ident[0:GT, 0:GT])
                last.then_inc(full["t1"], 1)

            def out1(g, half):
                ps = claim(pe, "B", "y1", 0, g) if half == 0 else bank_of("B", "y1")
                pe.wait_ge(drained["t1"], 2 * g + half + 1)
                for k in range(4 * half, 4 * half + 4):
                    last = mm(ps[0:GT, 0:D], o1t[:, k, :], o1w_t[:, k, :], k == 0, k == KO - 1)
                if half:
                    last.then_inc(full["y1"], 1)

            def xq_flip(g):
                ps = claim(pe, "B", "xqt", 0, g)[:, :].bitcast(BF16)
                pe.wait_ge(xq_ready, g + 1)
                for k in range(KD):
                    last = nc.tensor.transpose(ps[:, k * 112:k * 112 + GT], xq[:, k * 128:(k + 1) * 128], ident_b[0:GT, 0:GT])
                last.then_inc(full["xqt"], 1)

            def gate_up(g, u):
                ps = claim(pe, "B", "gu", u, g)
                if u == 0:
                    pe.wait_ge(drained["xqt"], g + 1)
                    pe.wait_ge(wq_ready, 3)
                w = (gate_q, up_q)[u % 2]
                for k in range(KD):
                    last = mm(ps[0:GT, :], xqt[:, k, :], w[:, k, (u // 2) * 512:(u // 2) * 512 + 512], k == 0, k == KD - 1)
                last.then_inc(full["gu"], 1)

            def hq_flip(g, u):
                ps = claim(pe, "B", "hqt", u, g)[:, :].bitcast(BF16)
                pe.wait_ge(hq_ready, 2 * g + u + 1)
                for i in range(4):
                    c = (4 * u + i) * 128
                    last = nc.tensor.transpose(ps[:, i * 112:i * 112 + GT], hq[:, c:c + 128], ident_b[0:GT, 0:GT])
                last.then_inc(full["hqt"], 1)

            def down(g):
                ps = claim(pe, "B", "down", 0, g)
                pe.wait_ge(drained["hqt"], 2 * g + 2)
                for k in range(KF):
                    last = mm(ps[0:GT, 0:D], hqt[:, k, :], down_q[:, k, :], k == 0, k == KF - 1)
                last.then_inc(full["down"], 1)

            def sum_sizes():
                pe.wait_ge(wabs_ready, 3)
                mm(bank_of("B", "xqt")[:, 0:3], ones[:, :], wabs[:, :]).then_inc(wsum_full, 1)

            def stage_a(g):
                embed(g)
                pe.wait_ge(w_in["l0"], 48)
                project0(g)
                values0(g)
                pe.wait_ge(tables_ready, 6)
                for j in range(QUADS):
                    scores0(g, j)
                for j in range(QUADS):
                    flip_probs(g, 0, j)
                for j in range(QUADS):
                    mix0(g, j)
                out0_flip(g)
                out0(g)
                sum_sizes()
                h1_flip(g)
                pe.wait_ge(w_in["moe"], 32)
                embed(g + 1)
                route(g)
                experts(g, 0)
                places(g)
                experts(g, 1)
                experts(g, 2)
                experts(g, 3)
                project0(g + 1)
                values0(g + 1)
                scores0(g + 1, 0)
                scores0(g + 1, 1)
                h2_flip(g)
                pe.wait_ge(w_in["qk1"], 16)
                pe.wait_ge(wmean_ready, 1)
                for u in range(3):
                    project1(g, u)

            def stage_b(g):
                project1(g, 3)
                values1(g, 0)
                for j in range(QUADS):
                    scores1(g, j)
                values1(g, 1)
                for j in range(QUADS):
                    flip_probs(g, 1, j)
                mix1(g, 0)
                mix1(g, 1)
                out1_flip(g, 0)
                mix1(g, 2)
                mix1(g, 3)
                out1(g, 0)
                out1_flip(g, 1)
                out1(g, 1)
                xq_flip(g)
                for u in range(4):
                    gate_up(g, u)
                for u in range(2):
                    hq_flip(g, u)
                down(g)

            def both(a, b, more=True):
                scores0(a, 2)
                scores0(a, 3)
                project1(b, 3)
                flip_probs(a, 0, 0)
                values1(b, 0)
                flip_probs(a, 0, 1)
                for j in range(QUADS):
                    scores1(b, j)
                    if j < 2:
                        flip_probs(a, 0, 2 + j)
                    mix0(a, j)
                values1(b, 1)
                for j in range(QUADS):
                    flip_probs(b, 1, j)
                out0_flip(a)
                mix1(b, 0)
                mix1(b, 1)
                out0(a)
                out1_flip(b, 0)
                mix1(b, 2)
                mix1(b, 3)
                out1(b, 0)
                out1_flip(b, 1)
                h1_flip(a)
                if more:
                    embed(a + 1, (0,))
                route(a)
                out1(b, 1)
                if more:
                    embed(a + 1, (1,))
                experts(a, 0)
                places(a)
                experts(a, 1)
                experts(a, 2)
                xq_flip(b)
                experts(a, 3)
                if more:
                    project0(a + 1)
                for u in range(4):
                    gate_up(b, u)
                if more:
                    values0(a + 1)
                    scores0(a + 1, 0)
                h2_flip(a)
                if more:
                    scores0(a + 1, 1)
                project1(a, 0)
                project1(a, 1)
                hq_flip(b, 0)
                hq_flip(b, 1)
                project1(a, 2)
                down(b)

            pe.wait_ge(w_in["const"], 64)
            pe.wait_ge(w_in["tok"], 16)
            stage_a(0)
            pe.wait_ge(w_in["v1"], 16)
            pe.wait_ge(w_in["o1"], 16)
            both(1, 0)
            with pe.Fori(2, NG - 1) as g:
                both(g, g - 1)
            both(NG - 1, NG - 2, more=False)
            stage_b(NG - 1)

        @block.scalar
        def _(act):
            def copy(o, i, scale=1.0):
                return nc.scalar.activation(o, i, ACT.Copy, scale=scale)

            def rows(ps, n):
                return ps[:, 0:n * GT].rearrange("p (k t) -> p k t", k=n)

            def keep_qk0(g):
                act.wait_ge(full["qk0"], g + 1)
                ps = rows(bank_of("A", "qk0"), 4)
                for par in range(2):
                    nc.scalar.activation(q0[:, par, :, :], ps[:, 0:2, :], ACT.Copy, scale=parity[:, par:par + 1])
                copy(k0[:, :, :], ps[:, 2:4, :]).then_inc(drained["qk0"], 1)

            def keep_v0(g):
                act.wait_ge(full["v0"], g + 1)
                ps = bank_of("A", "v0")
                copy(v0[:, :, 0:D0], ps[0:GT, 0:D].rearrange("p (h d) -> p h d", h=H)).then_inc(drained["v0"], 1)

            def exponentials(g, layer, j):
                act.wait_ge(shifted[layer], QUADS * g + j + 1)
                p = (p0, p1)[layer][:, 4 * j:4 * j + 4, :]
                nc.scalar.activation(p, p, ACT.Exp).then_inc(probs[layer], 1)

            def keep_flipped(g, layer, j):
                act.wait_ge(full[f"p{layer}"], QUADS * g + j + 1)
                ps = bank_of("AB"[layer], f"p{layer}", j)
                copy((p0t, p1t)[layer][:, 4 * j:4 * j + 4, :], rows(ps, 4)[0:GT]).then_inc(drained[f"p{layer}"], 1)

            def keep_rows(g, stage, kind, dst, n, u=0, per=1):
                act.wait_ge(full[kind], per * g + u + 1)
                copy(dst, rows(bank_of(stage, kind, u), n)).then_inc(drained[kind], 1)

            def keep_qk1(g, u):
                act.wait_ge(full["qk1"], 4 * g + u + 1)
                ps = rows(bank_of("B", "qk1", u), 4)
                dst = (q1, k1)[u % 2][:, 4 * (u // 2):4 * (u // 2) + 4, :]
                copy(dst, ps, D1 ** -0.5 if u % 2 == 0 else 1.0).then_inc(drained["qk1"], 1)

            def keep_v1(g, u):
                act.wait_ge(full["v1"], 2 * g + u + 1)
                ps = bank_of("B", "v1", u)
                copy(v1[:, 8 * u:8 * u + 8, 0:D1], ps[0:GT, :].rearrange("p (h d) -> p h d", h=8)).then_inc(drained["v1"], 1)

            def gap_exp(g):
                act.wait_ge(gap_ready, g + 1)
                nc.scalar.activation(egap[:, :], gap[:, :], ACT.Exp).then_inc(egap_ready, 1)

            def round_x(g):
                act.wait_ge(xscale_ready, g + 1)
                nc.scalar.activation(xr[:, :], h3[:, :], ACT.Identity, scale=xscale[:, :], bias=magic_t[0:GT, :]).then_inc(xr_ready, 1)

            def keep_xqt(g):
                act.wait_ge(full["xqt"], g + 1)
                ps = bank_of("B", "xqt")[:, :].bitcast(BF16)[:, 0:KD * 112].rearrange("p (k t) -> p k t", k=KD)
                copy(xqt[:, :, :], ps[:, :, 0:GT]).then_inc(drained["xqt"], 1)

            def relu_gate(g, half):
                act.wait_ge(full["gu"], 4 * g + 2 * half + 1)
                if later(g):
                    act.wait_ge(hid_ready, 2 * g)
                nc.scalar.activation(relu[:, half, :], bank_of("B", "gu", 2 * half)[0:GT, :], ACT.Relu).then_inc(relu_ready, 1)
                act.wait_ge(relu_ready, 2 * g + half + 1)
                nc.scalar.activation(relu[:, half, :], relu[:, half, :], ACT.Square).then_inc(relu2_ready, 1)

            def round_h1(g):
                act.wait_ge(hscale_ready, g + 1)
                nc.scalar.activation(hidr[:, 512:1024], hid[:, 1, :], ACT.Identity, scale=hscale[:, :],
                                     bias=magic_t[0:GT, :]).then_inc(hidr_ready, 1)

            def keep_hqt(g, u):
                act.wait_ge(full["hqt"], 2 * g + u + 1)
                ps = bank_of("B", "hqt", u)[:, :].bitcast(BF16)[:, 0:4 * 112].rearrange("p (k t) -> p k t", k=4)
                copy(hqt[:, 4 * u:4 * u + 4, :], ps[:, :, 0:GT]).then_inc(drained["hqt"], 1)

            def ternary_round(i):
                if i == 0:
                    act.wait_ge(winv_ready, 1)
                nc.scalar.activation(wff[:, i, :], wff[:, i, :], ACT.Identity, scale=winv[:, i:i + 1], bias=magic_t[:, :]).then_inc(wround, 1)

            def stage_a(g):
                keep_qk0(g)
                keep_v0(g)
                for j in range(QUADS):
                    exponentials(g, 0, j)
                for j in range(QUADS):
                    keep_flipped(g, 0, j)
                keep_rows(g, "A", "t0", o0t[:, :, :], KD)
                keep_rows(g, "A", "h1t", h1t[:, :, :], KD)
                ternary_round(0)
                gap_exp(g)
                ternary_round(1)
                ternary_round(2)
                keep_qk0(g + 1)
                keep_v0(g + 1)
                keep_rows(g, "B", "h2t", h2t[:, :, :], KD)
                for u in range(3):
                    keep_qk1(g, u)
                exponentials(g + 1, 0, 0)
                exponentials(g + 1, 0, 1)

            def stage_b(g):
                keep_qk1(g, 3)
                keep_v1(g, 0)
                for j in range(QUADS):
                    exponentials(g, 1, j)
                keep_v1(g, 1)
                for j in range(QUADS):
                    keep_flipped(g, 1, j)
                for u in range(2):
                    keep_rows(g, "B", "t1", o1t[:, 4 * u:4 * u + 4, :], 4, u, 2)
                round_x(g)
                keep_xqt(g)
                relu_gate(g, 0)
                relu_gate(g, 1)
                round_h1(g)
                keep_hqt(g, 0)
                keep_hqt(g, 1)

            def both(a, b, more=True):
                exponentials(a, 0, 2)
                keep_qk1(b, 3)
                keep_flipped(a, 0, 0)
                exponentials(a, 0, 3)
                keep_flipped(a, 0, 1)
                keep_v1(b, 0)
                for j in range(QUADS):
                    if j < 2:
                        keep_flipped(a, 0, 2 + j)
                    exponentials(b, 1, j)
                keep_v1(b, 1)
                for j in range(QUADS):
                    keep_flipped(b, 1, j)
                keep_rows(a, "A", "t0", o0t[:, :, :], KD)
                keep_rows(b, "B", "t1", o1t[:, 0:4, :], 4, 0, 2)
                keep_rows(b, "B", "t1", o1t[:, 4:8, :], 4, 1, 2)
                keep_rows(a, "A", "h1t", h1t[:, :, :], KD)
                gap_exp(a)
                round_x(b)
                keep_xqt(b)
                if more:
                    keep_qk0(a + 1)
                relu_gate(b, 0)
                relu_gate(b, 1)
                if more:
                    keep_v0(a + 1)
                keep_rows(a, "B", "h2t", h2t[:, :, :], KD)
                round_h1(b)
                keep_qk1(a, 0)
                keep_qk1(a, 1)
                keep_hqt(b, 0)
                keep_hqt(b, 1)
                keep_qk1(a, 2)
                if more:
                    exponentials(a + 1, 0, 0)
                    exponentials(a + 1, 0, 1)

            act.wait_ge(w_in["const"], 64)
            act.wait_ge(tables_ready, 6)
            stage_a(0)
            both(1, 0)
            with act.Fori(2, NG - 1) as g:
                both(g, g - 1)
            both(NG - 1, NG - 2, more=False)
            stage_b(NG - 1)

        @block.vector
        def _(dve):
            def keep_h0t(g):
                dve.wait_ge(full["tok"], g + 1)
                ps = bank_of("A", "tok")[:, 0:KD * GT].rearrange("p (k i s) -> p k i s", k=KD, i=IMG)
                for k in range(KD):
                    last = nc.vector.tensor_tensor(h0t[:, k, :].rearrange("p (i s) -> p i s", i=IMG), ps[:, k],
                                                   pos_t[:, k:k + 1, :].to_broadcast([128, IMG, S]), ALU.add)
                last.then_inc(drained["tok"], 1)

            def shift(g, layer, j):
                dve.wait_ge(full[f"s{layer}"], QUADS * g + j + 1)
                ps = bank_of("AB"[layer], f"s{layer}", j)[0:GT, 0:4 * GT].rearrange("p (h t) -> p h t", h=4)
                nm = (nmax0, nmax1)[layer][:, 4 * j:4 * j + 4]
                nc.vector.tensor_reduce(nm, ps, AX.X, ALU.max, negate=True).then_inc(nmax_ready[layer], 1)
                dve.wait_ge(nmax_ready[layer], QUADS * g + j + 1)
                nc.vector.tensor_tensor(
                    (p0, p1)[layer][:, 4 * j:4 * j + 4, :], ps, nm.unsqueeze(2).to_broadcast([GT, 4, GT]), ALU.add
                ).then_inc(shifted[layer], 1)
                dve.wait_ge(shifted[layer], QUADS * g + j + 1)

            def normalise(g, layer, j, heads, width, dst):
                kind = f"o{layer}"
                per = FILLS[kind]
                dve.wait_ge(full[kind], per * g + j + 1)
                ps = bank_of("AB"[layer], kind, j)[0:GT, 0:heads * (width + 1)].rearrange("p (h d) -> p h d", h=heads)
                rs = (rsum0, rsum1)[layer][:, heads * j:heads * (j + 1)]
                nc.vector.reciprocal(rs, ps[:, :, width]).then_inc(rsum_ready[layer], 1)
                dve.wait_ge(rsum_ready[layer], per * g + j + 1)
                nc.vector.tensor_tensor(dst.rearrange("p (h d) -> p h d", h=heads), ps[:, :, 0:width],
                                        rs.unsqueeze(2).to_broadcast([GT, heads, width]), ALU.mult).then_inc(drained[kind], 1)

            def variance(g, i, src):
                nc.vector.bn_stats(stats[:, i, :], src).then_inc(ln_stats[i], 1)
                dve.wait_ge(ln_stats[i], g + 1)
                dve.nop(nofuse=True)
                nc.vector.bn_aggr(mv[:, i, :], stats[:, i, :]).then_inc(ln_var[i], 1)

            def standardise(g, i, dst, src):
                dve.wait_ge(ln_var[i], g + 1)
                dve.wait_ge(ln_rstd[i], g + 1)
                return nc.vector.tensor_scalar(dst, src, mv[:, i, 0:1], rstd[:, i:i + 1], ALU.subtract, ALU.mult)

            def norm0_front(g):
                dve.wait_ge(full["y0"], g + 1)
                variance(g, 0, bank_of("A", "y0")[0:GT, 0:D])

            def norm0_back(g):
                standardise(g, 0, h1[:, :], bank_of("A", "y0")[0:GT, 0:D]).then_inc(h1_ready, 1)

            def choose(g):
                dve.wait_ge(full["logit"], g + 1)
                dve.nop(nofuse=True)
                lg = bank_of("A", "logit")[0:GT, 0:E]
                nc.vector.max(top[:, :], lg).then_inc(top_ready, 1)
                dve.wait_ge(top_ready, g + 1)
                dve.nop(nofuse=True)
                nc.vector.max_index(top_at[:, :], top[:, :], lg).then_inc(drained["logit"], 1)
                nc.vector.tensor_tensor(gap[:, :], top[:, 1:2], top[:, 0:1], ALU.subtract).then_inc(gap_ready, 1)
                dve.wait_ge(drained["logit"], g + 1)
                nc.vector.tensor_copy(top_atf[:, :], top_at[:, 0:2]).then_inc(atf_ready, 1)
                dve.wait_ge(atf_ready, g + 1)
                nc.vector.tensor_scalar(first[:, :], iota, top_atf[:, 0:1], None, ALU.is_equal).then_inc(onehot_ready, 1)
                nc.vector.tensor_scalar(second[:, :], iota, top_atf[:, 1:2], None, ALU.is_equal).then_inc(onehot_ready, 1)
                dve.wait_ge(onehot_ready, 2 * g + 2)
                nc.vector.tensor_tensor(chosen[:, :], first[:, :], second[:, :], ALU.add).then_inc(chosen_ready, 1)

            def gate_sum(g):
                dve.wait_ge(egap_ready, g + 1)
                nc.vector.tensor_scalar(esum[:, :], egap[:, :], 1.0, None, ALU.add).then_inc(esum_ready, 1)
                nc.vector.scalar_tensor_tensor(gate1[:, :], second[:, :], egap[:, :], first[:, :], ALU.mult, ALU.add).then_inc(gate1_ready, 1)

            def gate_share(g):
                dve.wait_ge(esum_ready, g + 1)
                nc.vector.reciprocal(share[:, :], esum[:, :]).then_inc(share_ready, 1)

            def gate_softmax(g):
                dve.wait_ge(share_ready, g + 1)
                dve.wait_ge(gate1_ready, g + 1)
                nc.vector.tensor_scalar(gate2[:, :], gate1[:, :], share[:, :], None, ALU.mult).then_inc(gate2_ready, 1)

            def gate_keep(g):
                dve.wait_ge(full["place"], g + 1)
                dve.wait_ge(gate2_ready, g + 1)
                nc.vector.scalar_tensor_tensor(gates[:, :], bank_of("A", "place")[0:GT, 0:E], float(CAP), gate2[:, :],
                                               ALU.is_lt, ALU.mult).then_inc(drained["place"], 1)

            def add_experts(g, u):
                dve.wait_ge(full["moe"], 4 * g + u + 1)
                if u == 0:
                    dve.wait_ge(drained["place"], g + 1)
                ps = bank_of("A", "moe", u)
                for i in range(2):
                    e = 2 * u + i
                    if e > 0:
                        dve.wait_ge(drained["moe"], E * g + e)
                    nc.vector.scalar_tensor_tensor(acc[:, :], ps[0:GT, i * D:(i + 1) * D], gates[:, e:e + 1],
                                                   (h1 if e == 0 else acc)[:, :], ALU.mult, ALU.add).then_inc(drained["moe"], 1)

            def norm1_front(g):
                dve.wait_ge(drained["moe"], E * g + E)
                variance(g, 1, acc[:, :])

            def norm1_back(g):
                standardise(g, 1, h2[:, :], acc[:, :]).then_inc(h2_ready, 1)

            def norm2_front(g):
                dve.wait_ge(full["y1"], g + 1)
                nc.vector.tensor_tensor(z1[:, :], bank_of("B", "y1")[0:GT, 0:D], h2[:, :], ALU.add).then_inc(drained["y1"], 1)
                dve.wait_ge(drained["y1"], g + 1)
                variance(g, 2, z1[:, :])

            def norm2_back(g):
                standardise(g, 2, h3[:, :], z1[:, :]).then_inc(h3_ready, 1)

            def x_max(g):
                dve.wait_ge(h3_ready, g + 1)
                nc.vector.tensor_reduce(xmax[:, :], h3[:, :], AX.X, ALU.max, apply_absolute_value=True).then_inc(xmax_ready, 1)

            def x_step(g):
                dve.wait_ge(xmax_ready, g + 1)
                nc.vector.tensor_scalar(xstep[:, :], xmax[:, :], EPS, 1.0 / 127.0, ALU.max, ALU.mult).then_inc(xstep_ready, 1)

            def x_scale(g):
                dve.wait_ge(xstep_ready, g + 1)
                nc.vector.reciprocal(xscale[:, :], xstep[:, :]).then_inc(xscale_ready, 1)

            def x_quantised(g):
                dve.wait_ge(xr_ready, g + 1)
                nc.vector.tensor_scalar(xq[:, :], xr[:, :], ROUND, 127.0, ALU.subtract, ALU.min).then_inc(xq_ready, 1)

            def h_step(g):
                nc.vector.tensor_tensor(xstep2[:, :], xstep[:, :], xstep[:, :], ALU.mult).then_inc(xstep2_ready, 1)
                dve.wait_ge(xstep2_ready, g + 1)
                nc.vector.scalar_tensor_tensor(hstep[:, :], xstep2[:, :], xstep[:, :], gu_size[0:GT, :], ALU.mult, ALU.mult).then_inc(hstep_ready, 1)

            def h_least(g):
                dve.wait_ge(hstep_ready, g + 1)
                nc.vector.tensor_scalar(hstep127[:, :], hstep[:, :], 127.0 / EPS, None, ALU.mult).then_inc(hstep127_ready, 1)
                dve.wait_ge(hstep127_ready, g + 1)
                nc.vector.reciprocal(hleast[:, :], hstep127[:, :]).then_inc(hleast_ready, 1)

            def hidden(g, half):
                dve.wait_ge(full["gu"], 4 * g + 2 * half + 2)
                dve.wait_ge(relu2_ready, 2 * g + half + 1)
                nc.vector.tensor_tensor(hid[:, half, :], relu[:, half, :], bank_of("B", "gu", 2 * half + 1)[0:GT, :], ALU.mult).then_inc(hid_ready, 1)
                dve.wait_ge(hid_ready, 2 * g + half + 1)
                nc.vector.tensor_reduce(hmax[:, half:half + 1], hid[:, half, :], AX.X, ALU.max, apply_absolute_value=True).then_inc(hmax_ready, 1)

            def h_size0(g):
                dve.wait_ge(hmax_ready, 2 * g + 1)
                dve.wait_ge(hleast_ready, g + 1)
                nc.vector.tensor_scalar(hmax0[:, :], hmax[:, 0:1], 1.0 / 127.0, hleast[:, :], ALU.mult, ALU.max).then_inc(hmax0_ready, 1)

            def h_scale(g):
                dve.wait_ge(hmax_ready, 2 * g + 2)
                dve.wait_ge(hmax0_ready, g + 1)
                nc.vector.tensor_scalar(hsize[:, :], hmax[:, 1:2], 1.0 / 127.0, hmax0[:, :], ALU.mult, ALU.max).then_inc(hsize_ready, 1)
                dve.wait_ge(hsize_ready, g + 1)
                nc.vector.reciprocal(hscale[:, :], hsize[:, :]).then_inc(hscale_ready, 1)

            def round_h0(g):
                dve.wait_ge(hscale_ready, g + 1)
                nc.vector.tensor_scalar(hidr[:, 0:512], hid[:, 0, :], hscale[:, :], ROUND, ALU.mult, ALU.add).then_inc(hidr0_ready, 1)

            def y_step(g):
                nc.vector.scalar_tensor_tensor(ystep[:, :], hsize[:, :], hstep[:, :], wmean[0:GT, 2:3], ALU.mult, ALU.mult).then_inc(ystep_ready, 1)

            def quantise_h(g, half):
                c = slice(half * 512, half * 512 + 512)
                dve.wait_ge((hidr0_ready, hidr_ready)[half], g + 1)
                nc.vector.tensor_scalar(hq[:, c], hidr[:, c], ROUND, 127.0, ALU.subtract, ALU.min).then_inc(hq_ready, 1)

            def norm3(g):
                dve.wait_ge(full["down"], g + 1)
                dve.wait_ge(ystep_ready, g + 1)
                nc.vector.scalar_tensor_tensor(z2[:, :], bank_of("B", "down")[0:GT, 0:D], ystep[:, :], h3[:, :],
                                               ALU.mult, ALU.add).then_inc(drained["down"], 1)
                dve.wait_ge(drained["down"], g + 1)
                variance(g, 3, z2[:, :])
                if later(g):
                    dve.wait_ge(out_done, 16 * g)
                standardise(g, 3, res[:, :], z2[:, :]).then_inc(out_ready, 1)

            def stage_a(g):
                keep_h0t(g)
                for j in range(QUADS):
                    shift(g, 0, j)
                ternary_sums()
                normalise(g, 0, 0, H, D0, o0[:, :])
                norm0_front(g)
                ternary_sizes()
                norm0_back(g)
                choose(g)
                gate_sum(g)
                gate_share(g)
                gate_softmax(g)
                keep_h0t(g + 1)
                ternary_clip(0)
                gate_keep(g)
                ternary_clip(1)
                for u in range(4):
                    add_experts(g, u)
                norm1_front(g)
                norm1_back(g)
                shift(g + 1, 0, 0)
                shift(g + 1, 0, 1)
                ternary_clip(2)
                dve.wait_ge(gu_size_ready, 1)

            def stage_b(g):
                for j in range(QUADS):
                    shift(g, 1, j)
                for j in range(QUADS):
                    normalise(g, 1, j, 4, D1, o1[:, 256 * j:256 * j + 256])
                norm2_front(g)
                norm2_back(g)
                x_max(g)
                x_step(g)
                x_scale(g)
                x_quantised(g)
                h_step(g)
                h_least(g)
                hidden(g, 0)
                h_size0(g)
                hidden(g, 1)
                h_scale(g)
                round_h0(g)
                y_step(g)
                quantise_h(g, 0)
                quantise_h(g, 1)
                norm3(g)

            def both(a, b, more=True):
                for j in range(2, QUADS):
                    shift(a, 0, j)
                for j in range(QUADS):
                    shift(b, 1, j)
                normalise(a, 0, 0, H, D0, o0[:, :])
                for j in range(2):
                    normalise(b, 1, j, 4, D1, o1[:, 256 * j:256 * j + 256])
                norm0_front(a)
                for j in range(2, 4):
                    normalise(b, 1, j, 4, D1, o1[:, 256 * j:256 * j + 256])
                norm0_back(a)
                choose(a)
                norm2_front(b)
                gate_sum(a)
                gate_share(a)
                gate_softmax(a)
                if more:
                    keep_h0t(a + 1)
                norm2_back(b)
                x_max(b)
                gate_keep(a)
                x_step(b)
                x_scale(b)
                add_experts(a, 0)
                x_quantised(b)
                h_step(b)
                h_least(b)
                add_experts(a, 1)
                add_experts(a, 2)
                add_experts(a, 3)
                norm1_front(a)
                norm1_back(a)
                hidden(b, 0)
                h_size0(b)
                hidden(b, 1)
                h_scale(b)
                round_h0(b)
                quantise_h(b, 0)
                quantise_h(b, 1)
                y_step(b)
                if more:
                    shift(a + 1, 0, 0)
                    shift(a + 1, 0, 1)
                norm3(b)

            def ternary_sums():
                dve.wait_ge(w_in["ff"], 48)
                for i in range(3):
                    nc.vector.tensor_reduce(wabs[:, i:i + 1], wff[:, i, :], AX.X, ALU.add, apply_absolute_value=True).then_inc(wabs_ready, 1)

            def ternary_sizes():
                dve.wait_ge(wsum_full, 1)
                nc.vector.tensor_scalar(wmean[:, :], bank_of("B", "xqt")[:, 0:3], 1.0 / (D * FF), EPS, ALU.mult, ALU.max).then_inc(wmean_ready, 1)
                dve.wait_ge(wmean_ready, 1)
                nc.vector.reciprocal(winv[:, :], wmean[:, :]).then_inc(winv_ready, 1)
                nc.vector.tensor_tensor(gu_sq[:, :], wmean[:, 0:1], wmean[:, 0:1], ALU.mult).then_inc(gu_sq_ready, 1)
                dve.wait_ge(gu_sq_ready, 1)
                nc.vector.tensor_tensor(gu_size[:, :], gu_sq[:, :], wmean[:, 1:2], ALU.mult).then_inc(gu_size_ready, 1)

            def ternary_clip(i):
                dve.wait_ge(wround, i + 1)
                nc.vector.tensor_scalar(wff[:, i, :], wff[:, i, :], ROUND + 1.0, ROUND - 1.0, ALU.min, ALU.max).then_inc(wclip, 1)

            dve.wait_ge(w_in["const"], 64)
            for k in range(KD):
                nc.vector.tensor_scalar(pos_t[:, k, 1:S], pos_t[:, k, 1:S], tokb_t[:, k:k + 1], None, ALU.add).then_inc(posb_sum, 1)
                nc.vector.tensor_scalar(pos_t[:, k, 0:1], pos_t[:, k, 0:1], cls_t[:, k:k + 1], None, ALU.add).then_inc(posb_sum, 1)
            nc.vector.tensor_copy(ident_b[:, :], ident).then_inc(tables_ready, 1)
            nc.vector.tensor_copy(mask_b[:, :, :], mask_f.unsqueeze(1).to_broadcast([GT, 4, GT])).then_inc(tables_ready, 1)
            nc.vector.tensor_copy(before_b[:, :], before_f).then_inc(tables_ready, 1)
            nc.vector.memset(eps_t[:, :], EPS).then_inc(tables_ready, 1)
            nc.vector.memset(magic_t[:, :], ROUND).then_inc(tables_ready, 1)
            nc.vector.memset(mhalf[:, :], -0.5).then_inc(tables_ready, 1)
            nc.vector.memset(v0[:, :, D0:D0 + 1], 1.0)
            nc.vector.memset(v1[:, :, D1:D1 + 1], 1.0)
            nc.vector.memset(ones[:, :], 1.0)
            dve.wait_ge(posb_sum, 2 * KD)
            stage_a(0)
            both(1, 0)
            with dve.Fori(2, NG - 1) as g:
                both(g, g - 1)
            both(NG - 1, NG - 2, more=False)
            stage_b(NG - 1)

        @block.gpsimd
        def _(pool):
            def deviation(g, i):
                pool.wait_ge(ln_var[i], g + 1)
                pool.nop(nofuse=True)
                nc.gpsimd.tensor_scalar(lnv[:, i:i + 1], mv[:, i, 1:2], EPS, None, ALU.add).then_inc(ln_log[i], 1)
                pool.wait_ge(ln_log[i], g + 1)
                nc.gpsimd.tensor_tensor(rstd[:, i:i + 1], lnv[:, i:i + 1], mhalf[0:GT, :], ALU.pow).then_inc(ln_rstd[i], 1)

            pool.wait_ge(tables_ready, 6)
            deviation(0, 0)
            deviation(0, 1)
            for i in range(3):
                pool.wait_ge(wclip, i + 1)
                nc.gpsimd.tensor_scalar(wq[:, i, :], wff[:, i, :], ROUND, None, ALU.subtract).then_inc(wq_ready, 1)
            with pool.Fori(1, NG) as g:
                deviation(g, 0)
                deviation(g - 1, 2)
                deviation(g, 1)
                deviation(g - 1, 3)
            deviation(NG - 1, 2)
            deviation(NG - 1, 3)


_ORDER = ["xp", "consts", "pos", "cls", "tokb", "tokw", "qk0w", "v0w", "o0w", "wr", "we", "qk1w", "v1w", "o1w", "wg", "wu", "wd"]


def kernel(**inputs):
    import concourse.bacc as _bacc
    from concourse.bass_utils import run_bass_kernel_spmd as _run

    a = {k: np.asarray(v) for k, v in inputs.items()}

    def rows(w, k):
        return np.ascontiguousarray(w.reshape(k, 128, -1).transpose(1, 0, 2))

    patches = a["x"].reshape(B, CH, PER_SIDE, PATCH, PER_SIDE, PATCH).transpose(0, 2, 4, 1, 3, 5).reshape(B, S - 1, PD)
    xs = np.zeros((NG * IMG, S, PD), patches.dtype)
    xs[:B, 1:] = patches
    xp = xs.reshape(NG, GT, KP, 128).transpose(0, 3, 2, 1)

    t = np.arange(GT)
    same = t[:, None] // S == t[None, :] // S
    consts = np.zeros((128, 128 + 2 * GT + 2 + E), np.float32)
    consts[:, 0:128] = np.eye(128)
    consts[:GT, 128:128 + GT] = np.where(same & (t[None, :] <= t[:, None]), 0.0, MASKED)
    consts[:GT, 128 + GT:128 + 2 * GT] = same & (t[:, None] < t[None, :])
    p = np.arange(128)
    for par in range(2):
        consts[:, 128 + 2 * GT + par] = np.where(p // D0 % 2 == par, D0 ** -0.5, 0.0)
    consts[:, 130 + 2 * GT:] = np.arange(E)

    heads0 = [4 * j + 2 * t_ + par for t_ in range(2) for j in range(4) for par in range(2)]
    cols0 = np.concatenate([np.arange(h * D0, (h + 1) * D0) for h in heads0])
    qk0 = np.concatenate([a["L0_attn_q_heads"].T[:, cols0], a["L0_attn_k_heads"].T[:, cols0]], 1)
    def pair(w, half):
        w = w.transpose(2, 0, 1)
        order = [8 * half + i + 4 * z for i in range(4) for z in range(2)]
        return w[:, order, :].reshape(D, -1)
    q, k = a["L1_attn_w_q"], a["L1_attn_w_k"]
    qk1 = np.concatenate([pair(q, 0), pair(k, 0), pair(q, 1), pair(k, 1)], 1)

    data = {
        "xp": xp, "consts": consts,
        "pos": a["L0_tok_pos_embedding"].reshape(S, KD, 128).transpose(2, 1, 0),
        "cls": a["L0_tok_cls_token"].reshape(KD, 128).T,
        "tokb": a["L0_tok_b"].reshape(KD, 128).T,
        "tokw": rows(a["L0_tok_W"].T, KP),
        "qk0w": rows(qk0, KD),
        "v0w": rows(a["L0_attn_v_heads"].T, KD),
        "o0w": rows(a["L0_attn_output_proj"].T, KD),
        "wr": rows(a["L0_ffn_Wr"].T, KD),
        "we": rows(a["L0_ffn_We"].transpose(1, 0, 2).reshape(D, E * D), KD),
        "qk1w": rows(qk1, KD),
        "v1w": rows(a["L1_attn_w_v"].transpose(2, 0, 1).reshape(D, W1), KD),
        "o1w": rows(a["L1_attn_w_o"], KO),
        "wg": rows(a["L1_ffn_w_gate"].T, KD).reshape(128, -1),
        "wu": rows(a["L1_ffn_w_up"].T, KD).reshape(128, -1),
        "wd": rows(a["L1_ffn_w_down"].T, KF).reshape(128, -1),
    }
    nc = _bacc.Bacc("TRN2", target_bir_lowering=False, num_devices=1)
    arrays, args = {}, []
    for name in _ORDER:
        v = np.ascontiguousarray(data[name])
        arrays[f"in_{name}"] = v
        args.append(nc.dram_tensor(f"in_{name}", v.shape, mybir.dt.from_np(v.dtype), kind="ExternalInput").ap())
    out = nc.dram_tensor("tokens_out", (NG, GT, D), F32, kind="ExternalOutput").ap()
    vit_tower(nc, *args, out)
    r = _run(nc, [arrays], core_ids=[0])
    return r.results[0]["tokens_out"].reshape(NG * IMG, S, D)[:B]
```

```python
from contextlib import ExitStack

import numpy as np
import concourse.bass as bass
from concourse import mybir

F32 = mybir.dt.float32
F32R = mybir.dt.float32r
BF16 = mybir.dt.bfloat16
U32 = mybir.dt.uint32
ALU = mybir.AluOpType
ACT = mybir.ActivationFunctionType
AX = mybir.AxisListType

B, SIDE, PATCH, CH = 32, 96, 16, 3
PER_SIDE = SIDE // PATCH
S = PER_SIDE * PER_SIDE + 1
D = 256
PD = CH * PATCH * PATCH
IMG = 3
GT = IMG * S
NG = -(-B // IMG)
KP = PD // 128
KD = D // 128
H = 16
QUADS = 4
D0 = D // H
D1 = 64
W1 = H * D1
KO = W1 // 128
E = 8
CAP = int(S * 2 / E * 1.5) + 1
FF = 1024
KF = FF // 128
EPS = 1e-5
MASKED = -1e30
WARM_UP = 20
WARM_NORM0, WARM_NORM2, WARM_HIDDEN = 14, 16, 8
ROUND = 1.5 * 2.0 ** 23


def fillings(kind, numbers, ahead=0):
    return [(kind, u, ahead) for u in numbers]


A_SLOTS = (fillings("s0", (3,)) + fillings("p0", range(QUADS)) + fillings("o0", (0,)) + fillings("t0", (0,))
           + fillings("y0", (0,)) + fillings("h1t", (0,)) + fillings("tok", (0,), 1) + fillings("logit", (0,))
           + fillings("moe", (0,)) + fillings("place", (0,)) + fillings("moe", (1, 2, 3)) + fillings("qk0", (0,), 1)
           + fillings("v0", (0,), 1) + fillings("s0", (0, 1, 2), 1))
B_SLOTS = (fillings("qk1", (3,)) + fillings("s1", (0, 1)) + fillings("v1", (0,)) + fillings("s1", (2, 3)) + fillings("v1", (1,))
           + fillings("p1", range(QUADS)) + fillings("o1", (0, 1)) + fillings("t1", (0,))
           + fillings("o1", (2, 3)) + fillings("y1", (0,)) + fillings("t1", (1,)) + fillings("xqt", (0,)) + fillings("gu", range(4)) + fillings("h2t", (0,), 1)
           + fillings("qk1", (0, 1), 1) + fillings("hqt", range(2)) + fillings("qk1", (2,), 1) + fillings("down", (0,)))
A_BANKS, B_BANKS = 3, 5
assert len(A_SLOTS) % A_BANKS == 0 and len(B_SLOTS) % B_BANKS == 0
KINDS = list(dict.fromkeys(k for k, _, _ in A_SLOTS + B_SLOTS))
FILLS = {k: [x for x, _, _ in A_SLOTS + B_SLOTS].count(k) for k in KINDS}


def vit_tower(nc, xp, consts, pos, cls, tokb, tokw, qk0w, v0w, o0w, wr, we, qk1w, v1w, o1w, wg, wu, wd, out):
    ctx = ExitStack()
    with ctx:
        def sb(name, shape, dt=F32):
            return ctx.enter_context(nc.sbuf_tensor(name, shape, dt))

        def sem(name):
            return ctx.enter_context(nc.semaphore(name))

        cst = sb("cst", [128, 128 + 2 * GT + 2 + E])
        ident = cst[:, 0:128]
        mask_f = cst[0:GT, 128:128 + GT]
        before_f = cst[0:GT, 128 + GT:128 + 2 * GT]
        parity = cst[:, 128 + 2 * GT:130 + 2 * GT]
        iota = cst[0:GT, 130 + 2 * GT:130 + 2 * GT + E]
        ident_b = sb("ident_b", [128, 128], BF16)
        before_b = sb("before_b", [GT, GT], BF16)
        ones = sb("ones", [128, 128])
        spare = sb("spare", [128, 1])
        mhalf = sb("mhalf", [128, 1])
        magic_t = sb("magic_t", [128, 1])
        pos_t = sb("pos_t", [128, KD, S])
        cls_t = sb("cls_t", [128, KD])
        tokb_t = sb("tokb_t", [128, KD])
        tokw_t = sb("tokw_t", [128, KP, D])
        qk0w_t = sb("qk0w_t", [128, KD, 2 * D])
        wr_t = sb("wr_t", [128, KD, E])
        qk1w_t = sb("qk1w_t", [128, KD, 2 * W1])
        v0w_part = [sb(f"v0w_{x}", [128, KD * D], F32R) for x in ("hi", "lo")]
        o0w_part = [sb(f"o0w_{x}", [128, KD * D], F32R) for x in ("hi", "lo")]
        we_part = [sb(f"we_{x}", [128, KD * E * D], F32R) for x in ("hi", "lo")]
        v1w_part = [sb(f"v1w_{x}", [128, KD * W1], F32R) for x in ("hi", "lo")]
        o1w_part = [sb(f"o1w_{x}", [128, KO * D], F32R) for x in ("hi", "lo")]
        v0w_hi, v0w_lo = [w[:, :].rearrange("p (k n) -> p k n", k=KD) for w in v0w_part]
        o0w_hi, o0w_lo = [w[:, :].rearrange("p (k n) -> p k n", k=KD) for w in o0w_part]
        we_hi, we_lo = [w[:, :].rearrange("p (k n) -> p k n", k=KD) for w in we_part]
        v1w_hi, v1w_lo = [w[:, :].rearrange("p (k n) -> p k n", k=KD) for w in v1w_part]
        o1w_hi, o1w_lo = [w[:, :].rearrange("p (k n) -> p k n", k=KO) for w in o1w_part]
        wq = sb("wq", [128, 3, 2048], BF16)
        gate_q = wq[:, 0, :].rearrange("p (k n) -> p k n", k=KD)
        up_q = wq[:, 1, :].rearrange("p (k n) -> p k n", k=KD)
        down_q = wq[:, 2, :].rearrange("p (k n) -> p k n", k=KF)
        wabs = sb("wabs", [128, 3])
        wmean = sb("wmean", [128, 3])
        winv = sb("winv", [128, 3])
        gu_sq = sb("gu_sq", [128, 1])
        gu_size = sb("gu_size", [128, 1])

        x_in = sb("x_in", [128, KP, GT])
        h0t = sb("h0t", [128, KD, GT])
        h0t_hi = sb("h0t_hi", [128, KD, GT], F32R)
        h0t_lo = sb("h0t_lo", [128, KD, GT], F32R)
        q0 = sb("q0", [128, 2, KD, GT])
        k0 = sb("k0", [128, KD, GT])
        v0 = sb("v0", [GT, H, D0 + 1])
        nmax0 = sb("nmax0", [GT, H])
        p0 = sb("p0", [GT, H, GT])
        p0t = sb("p0t", [GT, H, GT])
        rsum0 = sb("rsum0", [GT, H])
        o0 = sb("o0", [GT, D])
        o0t_hi = sb("o0t_hi", [128, KD, GT], F32R)
        o0t_lo = sb("o0t_lo", [128, KD, GT], F32R)
        h1 = sb("h1", [GT, D])
        h1t = sb("h1t", [128, KD, GT])
        h1t_hi = sb("h1t_hi", [128, KD, GT], F32R)
        h1t_lo = sb("h1t_lo", [128, KD, GT], F32R)
        logit = sb("logit", [GT, E])
        top = sb("top", [GT, 8])
        top_at = sb("top_at", [GT, 8], U32)
        top_atf = sb("top_atf", [GT, 2])
        first = sb("first", [GT, E])
        second = sb("second", [GT, E])
        chosen = sb("chosen", [GT, E], BF16)
        gap = sb("gap", [GT, 1])
        egap = sb("egap", [GT, 1])
        esum = sb("esum", [GT, 1])
        share = sb("share", [GT, 1])
        gate1 = sb("gate1", [GT, E])
        gate2 = sb("gate2", [GT, E])
        gates = sb("gates", [GT, E])
        acc = sb("acc", [GT, D])
        h2 = sb("h2", [GT, D])
        h2t = sb("h2t", [128, KD, GT])
        h2t_hi = sb("h2t_hi", [128, KD, GT], F32R)
        h2t_lo = sb("h2t_lo", [128, KD, GT], F32R)
        space1 = sb("space1", [128, 2 * H * GT + H * (D1 + 1) + W1 + 2 * 8 * GT])
        at = 0
        p1 = space1[0:GT, at:at + H * GT].rearrange("p (h t) -> p h t", h=H)
        at += H * GT
        p1t = space1[0:GT, at:at + H * GT].rearrange("p (h t) -> p h t", h=H)
        at += H * GT
        v1 = space1[0:GT, at:at + H * (D1 + 1)].rearrange("p (h d) -> p h d", h=H)
        at += H * (D1 + 1)
        o1 = space1[0:GT, at:at + W1]
        at += W1
        q1 = space1[:, at:at + 8 * GT].rearrange("p (k t) -> p k t", k=8)
        at += 8 * GT
        k1 = space1[:, at:at + 8 * GT].rearrange("p (k t) -> p k t", k=8)
        we_raw = space1[:, 0:4096]
        v1w_raw = space1[:, 4096:6144]
        v0w_raw = space1[:, 6144:6656]
        o0w_raw = space1[:, 6656:7168]
        up_raw = space1[:, 0:2048]
        down_raw = space1[:, 2048:4096]
        nmax1 = sb("nmax1", [GT, H])
        rsum1 = sb("rsum1", [GT, H])
        o1t_hi = sb("o1t_hi", [128, KO, GT], F32R)
        o1t_lo = sb("o1t_lo", [128, KO, GT], F32R)
        z1 = sb("z1", [GT, D])
        h3 = sb("h3", [GT, D])
        xmax = sb("xmax", [GT, 1])
        hleast = sb("hleast", [GT, 1])
        hstep127 = sb("hstep127", [GT, 1])
        xscale = sb("xscale", [GT, 1])
        xstep = sb("xstep", [GT, 1])
        xstep2 = sb("xstep2", [GT, 1])
        hstep = sb("hstep", [GT, 1])
        space2 = sb("space2", [128, 4096])
        relu = space2[0:GT, 0:1024].rearrange("p (u n) -> p u n", u=2)
        hid = space2[0:GT, 1024:2048].rearrange("p (u n) -> p u n", u=2)
        hidr = space2[0:GT, 2048:3072]
        hq = space2[0:GT, 3072:3584].bitcast(BF16)
        xr = space2[0:GT, 3584:3840]
        z2 = space2[0:GT, 3840:4096]
        o1w_raw = space2[:, 0:2048]
        gate_raw = space2[:, 2048:4096]
        ff_raw = (gate_raw, up_raw, down_raw)
        xq = sb("xq", [GT, D], BF16)
        xqt = sb("xqt", [128, KD, GT], BF16)
        hmax = sb("hmax", [GT, 2])
        hmax0 = sb("hmax0", [GT, 1])
        hsize = sb("hsize", [GT, 1])
        hscale = sb("hscale", [GT, 1])
        ystep = sb("ystep", [GT, 1])
        hqt = sb("hqt", [128, KF, GT], BF16)
        res = sb("res", [GT, D])
        stats = sb("stats", [GT, 4, 6])
        mv = sb("mv", [GT, 4, 2])
        var_eps = sb("var_eps", [GT, 4])
        rstd = sb("rstd", [GT, 4])

        banks = [ctx.enter_context(nc.psum_tensor(f"bank{i}", [128, 512], F32)) for i in range(8)]

        full = {k: sem("full_" + k) for k in KINDS}
        drained = {k: sem("drained_" + k) for k in KINDS if k not in ("s0", "s1", "y0", "gu")}
        w_in = {k: sem("in_" + k) for k in
                ["const", "tok", "qk0", "v0", "o0", "wr", "we", "qk1", "v1", "o1", "gate", "up", "down"]}
        part_hi, part_lo = sem("part_hi"), sem("part_lo")
        o1w_lo_ready, gate_q_ready = sem("o1w_lo_ready"), sem("gate_q_ready")
        w0_hi, w0_lo = sem("w0_hi"), sem("w0_lo")
        h0t_hi_ready, h0t_parts = sem("h0t_hi_ready"), sem("h0t_parts")
        h1t_parts, h2t_parts = sem("h1t_parts"), sem("h2t_parts")
        t0_hi, t1_hi = sem("t0_hi"), sem("t1_hi")
        x_ready = sem("x_ready")
        out_done = sem("out_done")
        pos_ready = sem("pos_ready")
        ones_ready = sem("ones_ready")
        tables_ready = sem("tables_ready")
        wabs_ready, wmean_ready = sem("wabs_ready"), sem("wmean_ready")
        winv_ready, gu_sq_ready, gu_size_ready = sem("winv_ready"), sem("gu_sq_ready"), sem("gu_size_ready")
        wclip, wround, wq_ready = sem("wclip"), sem("wround"), sem("wq_ready")
        wsum_full = sem("wsum_full")
        masked = [sem("masked0"), sem("masked1")]
        nmax_ready = [sem("nmax0_ready"), sem("nmax1_ready")]
        probs = [sem("probs0"), sem("probs1")]
        rsum_ready = [sem("rsum0_ready"), sem("rsum1_ready")]
        ln_stats = [sem(f"ln_stats{i}") for i in range(4)]
        ln_var = [sem(f"ln_var{i}") for i in range(4)]
        ln_shift = [sem(f"ln_shift{i}") for i in range(4)]
        ln_rstd = [sem(f"ln_rstd{i}") for i in range(4)]
        h1_ready, h2_ready, h3_ready, out_ready = sem("h1_ready"), sem("h2_ready"), sem("h3_ready"), sem("out_ready")
        z1_ready, z2_ready = sem("z1_ready"), sem("z2_ready")
        top_ready, at_ready, atf_ready = sem("top_ready"), sem("at_ready"), sem("atf_ready")
        onehot_ready, chosen_ready, gap_ready, egap_ready = sem("onehot_ready"), sem("chosen_ready"), sem("gap_ready"), sem("egap_ready")
        esum_ready, share_ready = sem("esum_ready"), sem("share_ready")
        gate1_ready, gate2_ready = sem("gate1_ready"), sem("gate2_ready")
        xmax_ready, xstep_ready, xscale_ready = sem("xmax_ready"), sem("xstep_ready"), sem("xscale_ready")
        hstep127_ready, hleast_ready = sem("hstep127_ready"), sem("hleast_ready")
        xstep2_ready, hstep_ready = sem("xstep2_ready"), sem("hstep_ready")
        xr_ready, xq_ready = sem("xr_ready"), sem("xq_ready")
        relu_ready, relu2_ready, hid_ready = sem("relu_ready"), sem("relu2_ready"), sem("hid_ready")
        hmax_ready, hmax0_ready, hsize_ready, hscale_ready = sem("hmax_ready"), sem("hmax0_ready"), sem("hsize_ready"), sem("hscale_ready")
        ystep_ready = sem("ystep_ready")
        hidr0_ready, hidr_ready, hq_ready = sem("hidr0_ready"), sem("hidr_ready"), sem("hq_ready")

        def bank_of(stage, kind, u=0):
            slots, n, base = (A_SLOTS, A_BANKS, 0) if stage == "A" else (B_SLOTS, B_BANKS, A_BANKS)
            return banks[base + [x[:2] for x in slots].index((kind, u)) % n]

        def drained_when(kind, u, g):
            if kind in ("s0", "s1"):
                return masked[int(kind[1])], QUADS * g + u + 1
            if kind == "y0":
                return h1_ready, g + 1
            if kind == "moe":
                return drained["moe"], E * g + 2 * u + 2
            if kind == "gu":
                return (relu_ready, hid_ready)[u % 2], 2 * g + u // 2 + 1
            return drained[kind], FILLS[kind] * g + u + 1

        def claim(pe, stage, kind, u, g):
            slots, n = (A_SLOTS, A_BANKS) if stage == "A" else (B_SLOTS, B_BANKS)
            at = [x[:2] for x in slots].index((kind, u))
            turn = g - slots[at][2]
            while True:
                at -= n
                if at < 0:
                    at, turn = at + len(slots), turn - 1
                k, v, ahead = slots[at]
                if not isinstance(g, int):
                    pe.wait_ge(*drained_when(k, v, turn + ahead))
                elif turn + ahead >= NG:
                    continue
                elif turn + ahead >= 0:
                    pe.wait_ge(*drained_when(k, v, turn + ahead))
                return bank_of(stage, kind, u)

        def later(g):
            return not (isinstance(g, int) and g == 0)

        block = ctx.enter_context(nc.Block())

        @block.sync
        def _(sp):
            sp.dma_start(cst[:, :], consts).then_inc(w_in["const"], 16)
            sp.dma_start(pos_t[:, :, :], pos).then_inc(w_in["const"], 16)
            sp.dma_start(cls_t[:, :], cls).then_inc(w_in["const"], 16)
            sp.dma_start(tokb_t[:, :], tokb).then_inc(w_in["const"], 16)
            sp.dma_start(tokw_t[:, :, :], tokw).then_inc(w_in["tok"], 16)
            sp.dma_start(x_in[:, :, :], xp[0]).then_inc(x_ready, 16)
            sp.dma_start(qk0w_t[:, :, :], qk0w).then_inc(w_in["qk0"], 16)
            sp.dma_start(v0w_raw, v0w).then_inc(w_in["v0"], 16)
            sp.dma_start(o0w_raw, o0w).then_inc(w_in["o0"], 16)
            sp.dma_start(wr_t[:, :, :], wr).then_inc(w_in["wr"], 16)
            sp.dma_start(we_raw, we).then_inc(w_in["we"], 16)
            sp.wait_ge(full["tok"], 1)
            sp.dma_start(x_in[:, :, :], xp[1]).then_inc(x_ready, 16)
            sp.dma_start(gate_raw, wg).then_inc(w_in["gate"], 16)
            sp.dma_start(v1w_raw, v1w).then_inc(w_in["v1"], 16)
            sp.dma_start(o1w_raw, o1w).then_inc(w_in["o1"], 16)
            sp.wait_ge(part_lo, 2)
            sp.dma_start(up_raw, wu).then_inc(w_in["up"], 16)
            sp.wait_ge(part_lo, 4)
            sp.dma_start(down_raw, wd).then_inc(w_in["down"], 16)
            sp.dma_start(qk1w_t[:, :, :], qk1w).then_inc(w_in["qk1"], 16)

            def store(g):
                sp.wait_ge(out_ready, g + 1)
                sp.dma_start(out[g], res[:, :]).then_inc(out_done, 16)

            with sp.Fori(1, NG - 1) as g:
                sp.wait_ge(full["tok"], g + 1)
                sp.dma_start(x_in[:, :, :], xp[g + 1]).then_inc(x_ready, 16)
                store(g - 1)
            store(NG - 2)
            store(NG - 1)
            sp.wait_ge(out_done, 16 * NG)

        @block.tensor
        def _(pe):
            def mm(o, l, r, first=True, last=True):
                return nc.tensor.matmul(o, l, r, start=first, stop=last)

            def mm_parts(o, l_hi, l_lo, r_hi, r_lo, first, last):
                mm(o, l_hi, r_hi, first, False)
                mm(o, l_hi, r_lo, False, False)
                return mm(o, l_lo, r_hi, False, last)

            def keep_warm(n, bank):
                for _ in range(n):
                    mm(bank[:, 0:128], ones[:, :], ones[:, :])

            def embed(g, halves=(0, 1)):
                if halves[0] == 0:
                    claim(pe, "A", "tok", 0, g)
                    pe.wait_ge(x_ready, 16 * g + 16)
                ps = bank_of("A", "tok")
                for m in halves:
                    for k in range(KP):
                        last = mm(ps[:, m * GT:(m + 1) * GT], tokw_t[:, k, m * 128:(m + 1) * 128], x_in[:, k, :],
                                  k == 0, k == KP - 1)
                if halves[-1] == KD - 1:
                    last.then_inc(full["tok"], 1)

            def project0(g, blocks=range(4)):
                if blocks[0] == 0:
                    claim(pe, "A", "qk0", 0, g)
                    pe.wait_ge(drained["tok"], g + 1)
                ps = bank_of("A", "qk0")
                for m in blocks:
                    for k in range(KD):
                        last = mm(ps[:, m * GT:(m + 1) * GT], qk0w_t[:, k, m * 128:(m + 1) * 128], h0t[:, k, :],
                                  k == 0, k == KD - 1)
                if blocks[-1] == 3:
                    last.then_inc(full["qk0"], 1)

            def values0(g):
                ps = claim(pe, "A", "v0", 0, g)
                pe.wait_ge(h0t_parts, g + 1)
                for k in range(KD):
                    last = mm_parts(ps[0:GT, 0:D], h0t_hi[:, k, :], h0t_lo[:, k, :], v0w_hi[:, k, :], v0w_lo[:, k, :],
                                    k == 0, k == KD - 1)
                last.then_inc(full["v0"], 1)

            def scores0(g, j):
                ps = claim(pe, "A", "s0", j, g)
                if j == 0:
                    pe.wait_ge(drained["qk0"], g + 1)
                for i in range(4):
                    r = slice(32 * j, 32 * j + 32)
                    last = mm(ps[0:GT, i * GT:(i + 1) * GT], q0[r, i % 2, i // 2, :], k0[r, i // 2, :])
                last.then_inc(full["s0"], 1)

            def flip_probs(g, layer, j):
                ps = claim(pe, "AB"[layer], f"p{layer}", j, g)
                pe.wait_ge(probs[layer], QUADS * g + j + 1)
                src = (p0, p1)[layer]
                for i in range(4):
                    last = nc.tensor.transpose(ps[0:GT, i * GT:(i + 1) * GT], src[:, 4 * j + i, :], ident[0:GT, 0:GT])
                last.then_inc(full[f"p{layer}"], 1)

            def mix0(g, j):
                if j == 0:
                    claim(pe, "A", "o0", 0, g)
                    pe.wait_ge(drained["v0"], g + 1)
                ps = bank_of("A", "o0")
                pe.wait_ge(drained["p0"], QUADS * g + j + 1)
                for h in range(4 * j, 4 * j + 4):
                    last = mm(ps[0:GT, h * (D0 + 1):(h + 1) * (D0 + 1)], p0t[:, h, :], v0[:, h, :])
                if j == QUADS - 1:
                    last.then_inc(full["o0"], 1)

            def out0_flip(g):
                ps = claim(pe, "A", "t0", 0, g)
                pe.wait_ge(drained["o0"], g + 1)
                for k in range(KD):
                    last = nc.tensor.transpose(ps[:, k * GT:(k + 1) * GT], o0[:, k * 128:(k + 1) * 128], ident[0:GT, 0:GT])
                last.then_inc(full["t0"], 1)

            def out0(g):
                ps = claim(pe, "A", "y0", 0, g)
                for k in range(KD):
                    mm(ps[0:GT, k * 128:(k + 1) * 128], h0t[:, k, :], ident, k == 0, False)
                pe.wait_ge(drained["t0"], g + 1)
                for k in range(KD):
                    last = mm_parts(ps[0:GT, 0:D], o0t_hi[:, k, :], o0t_lo[:, k, :], o0w_hi[:, k, :], o0w_lo[:, k, :],
                                    False, k == KD - 1)
                last.then_inc(full["y0"], 1)

            def h1_flip(g):
                ps = claim(pe, "A", "h1t", 0, g)
                pe.wait_ge(h1_ready, g + 1)
                for k in range(KD):
                    last = nc.tensor.transpose(ps[:, k * GT:(k + 1) * GT], h1[:, k * 128:(k + 1) * 128], ident[0:GT, 0:GT])
                last.then_inc(full["h1t"], 1)

            def route(g):
                ps = claim(pe, "A", "logit", 0, g)
                pe.wait_ge(drained["h1t"], g + 1)
                for k in range(KD):
                    last = mm(ps[0:GT, 0:E], h1t[:, k, :], wr_t[:, k, :], k == 0, k == KD - 1)
                last.then_inc(full["logit"], 1)

            def experts(g, u):
                ps = claim(pe, "A", "moe", u, g)
                if u == 0:
                    pe.wait_ge(h1t_parts, g + 1)
                c = slice(u * 512, (u + 1) * 512)
                for k in range(KD):
                    last = mm_parts(ps[0:GT, :], h1t_hi[:, k, :], h1t_lo[:, k, :], we_hi[:, k, c], we_lo[:, k, c],
                                    k == 0, k == KD - 1)
                last.then_inc(full["moe"], 1)

            def places(g):
                ps = claim(pe, "A", "place", 0, g)
                pe.wait_ge(chosen_ready, g + 1)
                mm(ps[0:GT, 0:E], before_b[:, :], chosen[:, :]).then_inc(full["place"], 1)

            def h2_flip(g):
                ps = claim(pe, "B", "h2t", 0, g)
                pe.wait_ge(h2_ready, g + 1)
                for k in range(KD):
                    last = nc.tensor.transpose(ps[:, k * GT:(k + 1) * GT], h2[:, k * 128:(k + 1) * 128], ident[0:GT, 0:GT])
                last.then_inc(full["h2t"], 1)

            def project1(g, u):
                ps = claim(pe, "B", "qk1", u, g)
                if u == 0:
                    pe.wait_ge(drained["h2t"], g + 1)
                for m in range(4):
                    for k in range(KD):
                        c = (4 * u + m) * 128
                        last = mm(ps[:, m * GT:(m + 1) * GT], qk1w_t[:, k, c:c + 128], h2t[:, k, :], k == 0, k == KD - 1)
                last.then_inc(full["qk1"], 1)

            def values1(g, u):
                ps = claim(pe, "B", "v1", u, g)
                if u == 0:
                    pe.wait_ge(h2t_parts, g + 1)
                c = slice(u * 512, (u + 1) * 512)
                for k in range(KD):
                    last = mm_parts(ps[0:GT, :], h2t_hi[:, k, :], h2t_lo[:, k, :], v1w_hi[:, k, c], v1w_lo[:, k, c],
                                    k == 0, k == KD - 1)
                last.then_inc(full["v1"], 1)

            def scores1(g, j):
                ps = claim(pe, "B", "s1", j, g)
                pe.wait_ge(drained["qk1"], 4 * g + 2 * (j // 2) + 2)
                r = slice(64 * (j % 2), 64 * (j % 2) + 64)
                for i in range(4):
                    t = 4 * (j // 2) + i
                    last = mm(ps[0:GT, i * GT:(i + 1) * GT], q1[r, t, :], k1[r, t, :])
                last.then_inc(full["s1"], 1)

            def mix1(g, j):
                ps = claim(pe, "B", "o1", j, g)
                if j == 0:
                    pe.wait_ge(drained["v1"], 2 * g + 2)
                pe.wait_ge(drained["p1"], QUADS * g + j + 1)
                for i in range(4):
                    h = 4 * j + i
                    last = mm(ps[0:GT, i * (D1 + 1):(i + 1) * (D1 + 1)], p1t[:, h, :], v1[:, h, :])
                last.then_inc(full["o1"], 1)

            def out1_flip(g, u):
                ps = claim(pe, "B", "t1", u, g)
                pe.wait_ge(drained["o1"], QUADS * g + 2 * u + 2)
                for i in range(4):
                    c = (4 * u + i) * 128
                    last = nc.tensor.transpose(ps[:, i * GT:(i + 1) * GT], o1[:, c:c + 128], ident[0:GT, 0:GT])
                last.then_inc(full["t1"], 1)

            def out1(g, half):
                if half == 0:
                    claim(pe, "B", "y1", 0, g)
                    pe.wait_ge(o1w_lo_ready, 1)
                ps = bank_of("B", "y1")
                pe.wait_ge(drained["t1"], 2 * g + half + 1)
                for k in range(4 * half, 4 * half + 4):
                    last = mm_parts(ps[0:GT, 0:D], o1t_hi[:, k, :], o1t_lo[:, k, :], o1w_hi[:, k, :], o1w_lo[:, k, :],
                                    k == 0, k == KO - 1)
                if half:
                    last.then_inc(full["y1"], 1)

            def xq_flip(g):
                ps = claim(pe, "B", "xqt", 0, g)[:, :].bitcast(BF16)
                pe.wait_ge(xq_ready, g + 1)
                for k in range(KD):
                    last = nc.tensor.transpose(ps[:, k * 112:k * 112 + GT], xq[:, k * 128:(k + 1) * 128], ident_b[0:GT, 0:GT])
                last.then_inc(full["xqt"], 1)

            def gate_up(g, u):
                ps = claim(pe, "B", "gu", u, g)
                if u == 0:
                    pe.wait_ge(drained["xqt"], g + 1)
                    pe.wait_ge(wq_ready, 2)
                    pe.wait_ge(gate_q_ready, 1)
                w = (gate_q, up_q)[u % 2]
                for k in range(KD):
                    last = mm(ps[0:GT, :], xqt[:, k, :], w[:, k, (u // 2) * 512:(u // 2) * 512 + 512], k == 0, k == KD - 1)
                last.then_inc(full["gu"], 1)

            def hq_flip(g, u):
                ps = claim(pe, "B", "hqt", u, g)[:, :].bitcast(BF16)
                pe.wait_ge(hq_ready, 2 * g + u + 1)
                for i in range(4):
                    c = (4 * u + i) * 128
                    last = nc.tensor.transpose(ps[:, i * 112:i * 112 + GT], hq[:, c:c + 128], ident_b[0:GT, 0:GT])
                last.then_inc(full["hqt"], 1)

            def down(g):
                ps = claim(pe, "B", "down", 0, g)
                pe.wait_ge(drained["hqt"], 2 * g + 2)
                for k in range(KF):
                    last = mm(ps[0:GT, 0:D], hqt[:, k, :], down_q[:, k, :], k == 0, k == KF - 1)
                last.then_inc(full["down"], 1)

            def sum_sizes():
                pe.wait_ge(wabs_ready, 3)
                mm(bank_of("B", "s1")[:, 0:3], ones[:, :], wabs[:, :]).then_inc(wsum_full, 1)

            def stage_a(g):
                embed(g)
                pe.wait_ge(w_in["qk0"], 16)
                project0(g)
                pe.wait_ge(w0_lo, 2)
                values0(g)
                pe.wait_ge(tables_ready, 4)
                for j in range(QUADS):
                    scores0(g, j)
                for j in range(QUADS):
                    flip_probs(g, 0, j)
                for j in range(QUADS):
                    mix0(g, j)
                out0_flip(g)
                out0(g)
                keep_warm(WARM_NORM0, bank_of("B", "v1"))
                h1_flip(g)
                embed(g + 1)
                pe.wait_ge(w_in["wr"], 16)
                route(g)
                pe.wait_ge(part_lo, 4)
                experts(g, 0)
                sum_sizes()
                places(g)
                experts(g, 1)
                experts(g, 2)
                experts(g, 3)
                project0(g + 1)
                values0(g + 1)
                scores0(g + 1, 0)
                scores0(g + 1, 1)
                h2_flip(g)
                scores0(g + 1, 2)
                pe.wait_ge(w_in["qk1"], 16)
                for u in range(3):
                    project1(g, u)

            def stage_b(g):
                project1(g, 3)
                scores1(g, 0)
                scores1(g, 1)
                values1(g, 0)
                scores1(g, 2)
                scores1(g, 3)
                values1(g, 1)
                for j in range(QUADS):
                    flip_probs(g, 1, j)
                mix1(g, 0)
                mix1(g, 1)
                out1_flip(g, 0)
                mix1(g, 2)
                mix1(g, 3)
                out1(g, 0)
                out1_flip(g, 1)
                out1(g, 1)
                keep_warm(WARM_NORM2, bank_of("A", "tok"))
                xq_flip(g)
                for u in range(4):
                    gate_up(g, u)
                keep_warm(WARM_HIDDEN, bank_of("A", "tok"))
                for u in range(2):
                    hq_flip(g, u)
                down(g)

            def both(a, b, more=True):
                scores0(a, 3)
                project1(b, 3)
                flip_probs(a, 0, 0)
                scores1(b, 0)
                flip_probs(a, 0, 1)
                scores1(b, 1)
                flip_probs(a, 0, 2)
                values1(b, 0)
                mix0(a, 0)
                scores1(b, 2)
                flip_probs(a, 0, 3)
                mix0(a, 1)
                scores1(b, 3)
                values1(b, 1)
                mix0(a, 2)
                flip_probs(b, 1, 0)
                flip_probs(b, 1, 1)
                mix0(a, 3)
                flip_probs(b, 1, 2)
                flip_probs(b, 1, 3)
                mix1(b, 0)
                out0_flip(a)
                mix1(b, 1)
                out0(a)
                out1_flip(b, 0)
                mix1(b, 2)
                mix1(b, 3)
                out1(b, 0)
                out1_flip(b, 1)
                h1_flip(a)
                if more:
                    embed(a + 1, (0,))
                route(a)
                if more:
                    embed(a + 1, (1,))
                experts(a, 0)
                places(a)
                out1(b, 1)
                experts(a, 1)
                experts(a, 2)
                experts(a, 3)
                if more:
                    project0(a + 1, (0, 1))
                xq_flip(b)
                if more:
                    project0(a + 1, (2, 3))
                for u in range(4):
                    gate_up(b, u)
                if more:
                    values0(a + 1)
                    scores0(a + 1, 0)
                    scores0(a + 1, 1)
                h2_flip(a)
                if more:
                    scores0(a + 1, 2)
                project1(a, 0)
                project1(a, 1)
                hq_flip(b, 0)
                hq_flip(b, 1)
                project1(a, 2)
                down(b)

            pe.wait_ge(ones_ready, 1)
            keep_warm(WARM_UP, bank_of("B", "v1"))
            pe.wait_ge(w_in["const"], 64)
            pe.wait_ge(w_in["tok"], 16)
            stage_a(0)
            pe.wait_ge(part_lo, 5)
            pe.wait_ge(wmean_ready, 1)
            both(1, 0)
            with pe.Fori(2, NG - 1) as g:
                both(g, g - 1)
            both(NG - 1, NG - 2, more=False)
            stage_b(NG - 1)

        @block.scalar
        def _(act):
            def copy(o, i, scale=1.0):
                return nc.scalar.activation(o, i, ACT.Copy, scale=scale)

            def rows(ps, n):
                return ps[:, 0:n * GT].rearrange("p (k t) -> p k t", k=n)

            def keep_qk0(g):
                act.wait_ge(full["qk0"], g + 1)
                ps = rows(bank_of("A", "qk0"), 4)
                for par in range(2):
                    nc.scalar.activation(q0[:, par, :, :], ps[:, 0:2, :], ACT.Copy, scale=parity[:, par:par + 1])
                copy(k0[:, :, :], ps[:, 2:4, :]).then_inc(drained["qk0"], 1)

            def keep_v0(g):
                act.wait_ge(full["v0"], g + 1)
                ps = bank_of("A", "v0")
                copy(v0[:, :, 0:D0], ps[0:GT, 0:D].rearrange("p (h d) -> p h d", h=H)).then_inc(drained["v0"], 1)

            def exponentials(g, layer, j):
                act.wait_ge(nmax_ready[layer], QUADS * g + j + 1)
                for h in range(4 * j, 4 * j + 4):
                    p = (p0, p1)[layer][:, h, :]
                    last = nc.scalar.activation(p, p, ACT.Exp, bias=(nmax0, nmax1)[layer][:, h:h + 1])
                last.then_inc(probs[layer], 1)

            def keep_flipped(g, layer, j):
                act.wait_ge(full[f"p{layer}"], QUADS * g + j + 1)
                ps = bank_of("AB"[layer], f"p{layer}", j)
                copy((p0t, p1t)[layer][:, 4 * j:4 * j + 4, :], rows(ps, 4)[0:GT]).then_inc(drained[f"p{layer}"], 1)

            def keep_o0t_hi(g):
                act.wait_ge(full["t0"], g + 1)
                copy(o0t_hi[:, :, :], rows(bank_of("A", "t0"), KD)).then_inc(t0_hi, 1)

            def keep_qk1(g, u):
                act.wait_ge(full["qk1"], 4 * g + u + 1)
                ps = rows(bank_of("B", "qk1", u), 4)
                dst = (q1, k1)[u % 2][:, 4 * (u // 2):4 * (u // 2) + 4, :]
                copy(dst, ps, D1 ** -0.5 if u % 2 == 0 else 1.0).then_inc(drained["qk1"], 1)

            def keep_v1(g, u):
                act.wait_ge(full["v1"], 2 * g + u + 1)
                ps = bank_of("B", "v1", u)
                copy(v1[:, 8 * u:8 * u + 8, 0:D1], ps[0:GT, :].rearrange("p (h d) -> p h d", h=8)).then_inc(drained["v1"], 1)

            def keep_flipped_rows(g, stage, kind, dst, hi):
                act.wait_ge(full[kind], g + 1)
                ps = rows(bank_of(stage, kind), KD)
                copy(dst, ps)
                copy(hi, ps).then_inc(drained[kind], 1)

            def keep_o1t_hi(g, u):
                act.wait_ge(full["t1"], 2 * g + u + 1)
                copy(o1t_hi[:, 4 * u:4 * u + 4, :], rows(bank_of("B", "t1", u), 4)).then_inc(t1_hi, 1)

            def weight_hi(w_hi, raw, c):
                copy(w_hi[:, c], raw[:, c]).then_inc(part_hi, 1)

            def gap_exp(g):
                act.wait_ge(gap_ready, g + 1)
                nc.scalar.activation(egap[:, :], gap[:, :], ACT.Exp).then_inc(egap_ready, 1)

            def round_x(g):
                act.wait_ge(xscale_ready, g + 1)
                nc.scalar.activation(xr[:, :], h3[:, :], ACT.Identity, scale=xscale[:, :], bias=magic_t[0:GT, :]).then_inc(xr_ready, 1)

            def keep_xqt(g):
                act.wait_ge(full["xqt"], g + 1)
                ps = bank_of("B", "xqt")[:, :].bitcast(BF16)[:, 0:KD * 112].rearrange("p (k t) -> p k t", k=KD)
                copy(xqt[:, :, :], ps[:, :, 0:GT]).then_inc(drained["xqt"], 1)

            def relu_gate(g, half):
                act.wait_ge(full["gu"], 4 * g + 2 * half + 1)
                if later(g):
                    act.wait_ge(hid_ready, 2 * g)
                nc.scalar.activation(relu[:, half, :], bank_of("B", "gu", 2 * half)[0:GT, :], ACT.Relu).then_inc(relu_ready, 1)
                act.wait_ge(relu_ready, 2 * g + half + 1)
                nc.scalar.activation(relu[:, half, :], relu[:, half, :], ACT.Square).then_inc(relu2_ready, 1)

            def round_h1(g):
                act.wait_ge(hscale_ready, g + 1)
                nc.scalar.activation(hidr[:, 512:1024], hid[:, 1, :], ACT.Identity, scale=hscale[:, :],
                                     bias=magic_t[0:GT, :]).then_inc(hidr_ready, 1)

            def keep_hqt(g, u):
                act.wait_ge(full["hqt"], 2 * g + u + 1)
                ps = bank_of("B", "hqt", u)[:, :].bitcast(BF16)[:, 0:4 * 112].rearrange("p (k t) -> p k t", k=4)
                copy(hqt[:, 4 * u:4 * u + 4, :], ps[:, :, 0:GT]).then_inc(drained["hqt"], 1)

            def ternary_round(i):
                act.wait_ge(winv_ready, 1)
                nc.scalar.activation(ff_raw[i], ff_raw[i], ACT.Identity, scale=winv[:, i:i + 1], bias=magic_t[:, :]).then_inc(wround, 1)

            def stage_a(g):
                keep_qk0(g)
                keep_v0(g)
                act.wait_ge(w_in["we"], 16)
                weight_hi(we_part[0], we_raw, slice(0, 1024))
                for j in range(QUADS):
                    exponentials(g, 0, j)
                for j in range(QUADS):
                    keep_flipped(g, 0, j)
                for j in range(1, QUADS):
                    weight_hi(we_part[0], we_raw, slice(1024 * j, 1024 * j + 1024))
                act.wait_ge(w_in["v1"], 16)
                weight_hi(v1w_part[0], v1w_raw, slice(0, 2048))
                keep_o0t_hi(g)
                act.wait_ge(w_in["o1"], 16)
                weight_hi(o1w_part[0], o1w_raw, slice(0, 2048))
                keep_flipped_rows(g, "A", "h1t", h1t[:, :, :], h1t_hi[:, :, :])
                gap_exp(g)
                ternary_round(1)
                ternary_round(2)
                keep_qk0(g + 1)
                keep_v0(g + 1)
                keep_flipped_rows(g, "B", "h2t", h2t[:, :, :], h2t_hi[:, :, :])
                act.wait_ge(part_lo, 5)
                keep_qk1(g, 0)
                ternary_round(0)
                keep_qk1(g, 1)
                keep_qk1(g, 2)
                for j in range(3):
                    exponentials(g + 1, 0, j)

            def stage_b(g):
                keep_qk1(g, 3)
                keep_v1(g, 0)
                for j in range(QUADS):
                    exponentials(g, 1, j)
                keep_v1(g, 1)
                for j in range(QUADS):
                    keep_flipped(g, 1, j)
                for u in range(2):
                    keep_o1t_hi(g, u)
                round_x(g)
                keep_xqt(g)
                relu_gate(g, 0)
                relu_gate(g, 1)
                round_h1(g)
                keep_hqt(g, 0)
                keep_hqt(g, 1)

            def both(a, b, more=True):
                keep_qk1(b, 3)
                keep_flipped(a, 0, 0)
                keep_flipped(a, 0, 1)
                exponentials(a, 0, 3)
                exponentials(b, 1, 0)
                keep_flipped(a, 0, 2)
                exponentials(b, 1, 1)
                keep_v1(b, 0)
                keep_flipped(a, 0, 3)
                exponentials(b, 1, 2)
                exponentials(b, 1, 3)
                keep_v1(b, 1)
                for j in range(QUADS):
                    keep_flipped(b, 1, j)
                keep_o0t_hi(a)
                keep_o1t_hi(b, 0)
                keep_o1t_hi(b, 1)
                keep_flipped_rows(a, "A", "h1t", h1t[:, :, :], h1t_hi[:, :, :])
                gap_exp(a)
                round_x(b)
                keep_xqt(b)
                if more:
                    keep_qk0(a + 1)
                relu_gate(b, 0)
                relu_gate(b, 1)
                if more:
                    keep_v0(a + 1)
                keep_flipped_rows(a, "B", "h2t", h2t[:, :, :], h2t_hi[:, :, :])
                round_h1(b)
                keep_qk1(a, 0)
                keep_qk1(a, 1)
                keep_hqt(b, 0)
                keep_hqt(b, 1)
                keep_qk1(a, 2)
                if more:
                    for j in range(3):
                        exponentials(a + 1, 0, j)

            act.wait_ge(ones_ready, 1)
            nc.scalar.activation(spare[:, :], ones[:, 0:1], ACT.Exp)
            act.wait_ge(w_in["v0"], 16)
            copy(v0w_part[0][:, :], v0w_raw).then_inc(w0_hi, 1)
            act.wait_ge(w_in["o0"], 16)
            copy(o0w_part[0][:, :], o0w_raw).then_inc(w0_hi, 1)
            act.wait_ge(w_in["const"], 64)
            act.wait_ge(tables_ready, 4)
            stage_a(0)
            both(1, 0)
            with act.Fori(2, NG - 1) as g:
                both(g, g - 1)
            both(NG - 1, NG - 2, more=False)
            stage_b(NG - 1)

        @block.vector
        def _(dve):
            def keep_h0t(g):
                dve.wait_ge(full["tok"], g + 1)
                ps = bank_of("A", "tok")[:, 0:KD * GT].rearrange("p (k i s) -> p k i s", k=KD, i=IMG)
                for k in range(KD):
                    last = nc.vector.tensor_tensor(h0t[:, k, :].rearrange("p (i s) -> p i s", i=IMG), ps[:, k],
                                                   pos_t[:, k:k + 1, :].to_broadcast([128, IMG, S]), ALU.add)
                last.then_inc(drained["tok"], 1)

            def row_max(g, layer, j):
                dve.wait_ge(full[f"s{layer}"], QUADS * g + j + 1)
                ps = bank_of("AB"[layer], f"s{layer}", j)[0:GT, 0:4 * GT].rearrange("p (h t) -> p h t", h=4)
                p = (p0, p1)[layer][:, 4 * j:4 * j + 4, :]
                nc.vector.tensor_tensor(p, ps, mask_f.unsqueeze(1).to_broadcast([GT, 4, GT]), ALU.add).then_inc(masked[layer], 1)
                dve.wait_ge(masked[layer], QUADS * g + j + 1)
                nc.vector.tensor_reduce((nmax0, nmax1)[layer][:, 4 * j:4 * j + 4], p, AX.X, ALU.max,
                                        negate=True).then_inc(nmax_ready[layer], 1)

            def normalise(g, layer, j, heads, width, dst):
                kind = f"o{layer}"
                per = FILLS[kind]
                dve.wait_ge(full[kind], per * g + j + 1)
                ps = bank_of("AB"[layer], kind, j)[0:GT, 0:heads * (width + 1)].rearrange("p (h d) -> p h d", h=heads)
                rs = (rsum0, rsum1)[layer][:, heads * j:heads * (j + 1)]
                nc.vector.reciprocal(rs, ps[:, :, width]).then_inc(rsum_ready[layer], 1)
                dve.wait_ge(rsum_ready[layer], per * g + j + 1)
                nc.vector.tensor_tensor(dst.rearrange("p (h d) -> p h d", h=heads), ps[:, :, 0:width],
                                        rs.unsqueeze(2).to_broadcast([GT, heads, width]), ALU.mult).then_inc(drained[kind], 1)

            def variance(g, i, src):
                nc.vector.bn_stats(stats[:, i, :], src).then_inc(ln_stats[i], 1)
                dve.wait_ge(ln_stats[i], g + 1)
                dve.nop(nofuse=True)
                nc.vector.bn_aggr(mv[:, i, :], stats[:, i, :]).then_inc(ln_var[i], 1)

            def standardise(g, i, dst, src):
                dve.wait_ge(ln_var[i], g + 1)
                dve.wait_ge(ln_rstd[i], g + 1)
                return nc.vector.tensor_scalar(dst, src, mv[:, i, 0:1], rstd[:, i:i + 1], ALU.subtract, ALU.mult)

            def o0t_low(g):
                dve.wait_ge(t0_hi, g + 1)
                ps = bank_of("A", "t0")[:, 0:KD * GT].rearrange("p (k t) -> p k t", k=KD)
                nc.vector.tensor_tensor(o0t_lo[:, :, :], ps, o0t_hi[:, :, :].bitcast(F32), ALU.subtract).then_inc(drained["t0"], 1)

            def o1t_low(g, u):
                dve.wait_ge(t1_hi, 2 * g + u + 1)
                c = slice(4 * u, 4 * u + 4)
                ps = bank_of("B", "t1", u)[:, 0:4 * GT].rearrange("p (k t) -> p k t", k=4)
                nc.vector.tensor_tensor(o1t_lo[:, c, :], ps, o1t_hi[:, c, :].bitcast(F32), ALU.subtract).then_inc(drained["t1"], 1)

            def weight_lo(number, parts, raw, c):
                dve.wait_ge(part_hi, number)
                nc.vector.tensor_tensor(parts[1][:, c], raw[:, c], parts[0][:, c].bitcast(F32), ALU.subtract).then_inc(part_lo, 1)

            def we_lo_chunk(j):
                weight_lo(j + 1, we_part, we_raw, slice(1024 * j, 1024 * j + 1024))

            def norm0_front(g):
                dve.wait_ge(full["y0"], g + 1)
                variance(g, 0, bank_of("A", "y0")[0:GT, 0:D])

            def norm0_back(g):
                standardise(g, 0, h1[:, :], bank_of("A", "y0")[0:GT, 0:D]).then_inc(h1_ready, 1)

            def choose(g):
                dve.wait_ge(full["logit"], g + 1)
                dve.nop(nofuse=True)
                lg = bank_of("A", "logit")[0:GT, 0:E]
                nc.vector.max(top[:, :], lg).then_inc(top_ready, 1)
                dve.wait_ge(top_ready, g + 1)
                dve.nop(nofuse=True)
                nc.vector.max_index(top_at[:, :], top[:, :], lg).then_inc(drained["logit"], 1)
                nc.vector.tensor_tensor(gap[:, :], top[:, 1:2], top[:, 0:1], ALU.subtract).then_inc(gap_ready, 1)
                dve.wait_ge(drained["logit"], g + 1)
                nc.vector.tensor_copy(top_atf[:, :], top_at[:, 0:2]).then_inc(atf_ready, 1)
                dve.wait_ge(atf_ready, g + 1)
                nc.vector.tensor_scalar(first[:, :], iota, top_atf[:, 0:1], None, ALU.is_equal).then_inc(onehot_ready, 1)
                nc.vector.tensor_scalar(second[:, :], iota, top_atf[:, 1:2], None, ALU.is_equal).then_inc(onehot_ready, 1)
                dve.wait_ge(onehot_ready, 2 * g + 2)
                nc.vector.tensor_tensor(chosen[:, :], first[:, :], second[:, :], ALU.add).then_inc(chosen_ready, 1)

            def gate_sum(g):
                dve.wait_ge(egap_ready, g + 1)
                nc.vector.tensor_scalar(esum[:, :], egap[:, :], 1.0, None, ALU.add).then_inc(esum_ready, 1)
                nc.vector.scalar_tensor_tensor(gate1[:, :], second[:, :], egap[:, :], first[:, :], ALU.mult, ALU.add).then_inc(gate1_ready, 1)

            def gate_share(g):
                dve.wait_ge(esum_ready, g + 1)
                nc.vector.reciprocal(share[:, :], esum[:, :]).then_inc(share_ready, 1)

            def gate_softmax(g):
                dve.wait_ge(share_ready, g + 1)
                dve.wait_ge(gate1_ready, g + 1)
                nc.vector.tensor_scalar(gate2[:, :], gate1[:, :], share[:, :], None, ALU.mult).then_inc(gate2_ready, 1)

            def gate_keep(g):
                dve.wait_ge(full["place"], g + 1)
                dve.wait_ge(gate2_ready, g + 1)
                nc.vector.scalar_tensor_tensor(gates[:, :], bank_of("A", "place")[0:GT, 0:E], float(CAP), gate2[:, :],
                                               ALU.is_lt, ALU.mult).then_inc(drained["place"], 1)

            def add_experts(g, u):
                dve.wait_ge(full["moe"], 4 * g + u + 1)
                if u == 0:
                    dve.wait_ge(drained["place"], g + 1)
                ps = bank_of("A", "moe", u)
                for i in range(2):
                    e = 2 * u + i
                    if e > 0:
                        dve.wait_ge(drained["moe"], E * g + e)
                    nc.vector.scalar_tensor_tensor(acc[:, :], ps[0:GT, i * D:(i + 1) * D], gates[:, e:e + 1],
                                                   (h1 if e == 0 else acc)[:, :], ALU.mult, ALU.add).then_inc(drained["moe"], 1)

            def norm1_front(g):
                dve.wait_ge(drained["moe"], E * g + E)
                variance(g, 1, acc[:, :])

            def norm1_back(g):
                standardise(g, 1, h2[:, :], acc[:, :]).then_inc(h2_ready, 1)

            def norm2_front(g):
                dve.wait_ge(full["y1"], g + 1)
                nc.vector.tensor_tensor(z1[:, :], bank_of("B", "y1")[0:GT, 0:D], h2[:, :], ALU.add).then_inc(drained["y1"], 1)
                dve.wait_ge(drained["y1"], g + 1)
                variance(g, 2, z1[:, :])

            def norm2_back(g):
                standardise(g, 2, h3[:, :], z1[:, :]).then_inc(h3_ready, 1)

            def x_max(g):
                dve.wait_ge(h3_ready, g + 1)
                nc.vector.tensor_reduce(xmax[:, :], h3[:, :], AX.X, ALU.max, apply_absolute_value=True).then_inc(xmax_ready, 1)

            def x_step(g):
                dve.wait_ge(xmax_ready, g + 1)
                nc.vector.tensor_scalar(xstep[:, :], xmax[:, :], EPS, 1.0 / 127.0, ALU.max, ALU.mult).then_inc(xstep_ready, 1)

            def x_scale(g):
                dve.wait_ge(xstep_ready, g + 1)
                nc.vector.reciprocal(xscale[:, :], xstep[:, :]).then_inc(xscale_ready, 1)

            def x_quantised(g):
                dve.wait_ge(xr_ready, g + 1)
                nc.vector.tensor_scalar(xq[:, :], xr[:, :], ROUND, 127.0, ALU.subtract, ALU.min).then_inc(xq_ready, 1)

            def h_step(g):
                nc.vector.tensor_tensor(xstep2[:, :], xstep[:, :], xstep[:, :], ALU.mult).then_inc(xstep2_ready, 1)
                dve.wait_ge(xstep2_ready, g + 1)
                nc.vector.scalar_tensor_tensor(hstep[:, :], xstep2[:, :], xstep[:, :], gu_size[0:GT, :], ALU.mult, ALU.mult).then_inc(hstep_ready, 1)

            def h_least(g):
                dve.wait_ge(hstep_ready, g + 1)
                nc.vector.tensor_scalar(hstep127[:, :], hstep[:, :], 127.0 / EPS, None, ALU.mult).then_inc(hstep127_ready, 1)
                dve.wait_ge(hstep127_ready, g + 1)
                nc.vector.reciprocal(hleast[:, :], hstep127[:, :]).then_inc(hleast_ready, 1)

            def hidden(g, half):
                dve.wait_ge(full["gu"], 4 * g + 2 * half + 2)
                dve.wait_ge(relu2_ready, 2 * g + half + 1)
                nc.vector.tensor_tensor(hid[:, half, :], relu[:, half, :], bank_of("B", "gu", 2 * half + 1)[0:GT, :], ALU.mult).then_inc(hid_ready, 1)
                dve.wait_ge(hid_ready, 2 * g + half + 1)
                nc.vector.tensor_reduce(hmax[:, half:half + 1], hid[:, half, :], AX.X, ALU.max, apply_absolute_value=True).then_inc(hmax_ready, 1)

            def h_size0(g):
                dve.wait_ge(hmax_ready, 2 * g + 1)
                dve.wait_ge(hleast_ready, g + 1)
                nc.vector.tensor_scalar(hmax0[:, :], hmax[:, 0:1], 1.0 / 127.0, hleast[:, :], ALU.mult, ALU.max).then_inc(hmax0_ready, 1)

            def h_scale(g):
                dve.wait_ge(hmax_ready, 2 * g + 2)
                dve.wait_ge(hmax0_ready, g + 1)
                nc.vector.tensor_scalar(hsize[:, :], hmax[:, 1:2], 1.0 / 127.0, hmax0[:, :], ALU.mult, ALU.max).then_inc(hsize_ready, 1)
                dve.wait_ge(hsize_ready, g + 1)
                nc.vector.reciprocal(hscale[:, :], hsize[:, :]).then_inc(hscale_ready, 1)

            def round_h0(g):
                dve.wait_ge(hscale_ready, g + 1)
                nc.vector.tensor_scalar(hidr[:, 0:512], hid[:, 0, :], hscale[:, :], ROUND, ALU.mult, ALU.add).then_inc(hidr0_ready, 1)

            def y_step(g):
                nc.vector.scalar_tensor_tensor(ystep[:, :], hsize[:, :], hstep[:, :], wmean[0:GT, 2:3], ALU.mult, ALU.mult).then_inc(ystep_ready, 1)

            def quantise_h(g, half):
                c = slice(half * 512, half * 512 + 512)
                dve.wait_ge((hidr0_ready, hidr_ready)[half], g + 1)
                nc.vector.tensor_scalar(hq[:, c], hidr[:, c], ROUND, 127.0, ALU.subtract, ALU.min).then_inc(hq_ready, 1)

            def norm3(g):
                dve.wait_ge(full["down"], g + 1)
                dve.wait_ge(ystep_ready, g + 1)
                nc.vector.scalar_tensor_tensor(z2[:, :], bank_of("B", "down")[0:GT, 0:D], ystep[:, :], h3[:, :],
                                               ALU.mult, ALU.add).then_inc(drained["down"], 1)
                dve.wait_ge(drained["down"], g + 1)
                variance(g, 3, z2[:, :])
                if later(g):
                    dve.wait_ge(out_done, 16 * g)
                standardise(g, 3, res[:, :], z2[:, :]).then_inc(out_ready, 1)

            def stage_a(g):
                keep_h0t(g)
                for i, (parts, raw) in enumerate(((v0w_part, v0w_raw), (o0w_part, o0w_raw))):
                    dve.wait_ge(w0_hi, i + 1)
                    nc.vector.tensor_tensor(parts[1][:, :], raw, parts[0][:, :].bitcast(F32), ALU.subtract).then_inc(w0_lo, 1)
                for j in range(QUADS):
                    row_max(g, 0, j)
                we_lo_chunk(0)
                ternary_sum(0, "gate")
                for j in range(1, 4):
                    we_lo_chunk(j)
                normalise(g, 0, 0, H, D0, o0[:, :])
                o0t_low(g)
                ternary_sum(1, "up")
                norm0_front(g)
                norm0_back(g)
                ternary_sum(2, "down")
                choose(g)
                gate_sum(g)
                gate_share(g)
                gate_softmax(g)
                keep_h0t(g + 1)
                gate_keep(g)
                ternary_sizes()
                for u in range(4):
                    add_experts(g, u)
                norm1_front(g)
                norm1_back(g)
                weight_lo(5, v1w_part, v1w_raw, slice(0, 2048))
                for j in range(3):
                    row_max(g + 1, 0, j)
                ternary_keep(1)
                ternary_keep(2)
                ternary_keep(0)

            def stage_b(g):
                for j in range(QUADS):
                    row_max(g, 1, j)
                for j in range(2):
                    normalise(g, 1, j, 4, D1, o1[:, 256 * j:256 * j + 256])
                o1t_low(g, 0)
                for j in range(2, QUADS):
                    normalise(g, 1, j, 4, D1, o1[:, 256 * j:256 * j + 256])
                o1t_low(g, 1)
                norm2_front(g)
                norm2_back(g)
                x_max(g)
                x_step(g)
                x_scale(g)
                x_quantised(g)
                h_step(g)
                h_least(g)
                hidden(g, 0)
                h_size0(g)
                hidden(g, 1)
                h_scale(g)
                round_h0(g)
                y_step(g)
                quantise_h(g, 0)
                quantise_h(g, 1)
                norm3(g)

            def both(a, b, more=True):
                row_max(a, 0, 3)
                for j in range(QUADS):
                    row_max(b, 1, j)
                normalise(a, 0, 0, H, D0, o0[:, :])
                normalise(b, 1, 0, 4, D1, o1[:, 0:256])
                o0t_low(a)
                normalise(b, 1, 1, 4, D1, o1[:, 256:512])
                norm0_front(a)
                o1t_low(b, 0)
                for j in range(2, 4):
                    normalise(b, 1, j, 4, D1, o1[:, 256 * j:256 * j + 256])
                norm0_back(a)
                o1t_low(b, 1)
                choose(a)
                gate_sum(a)
                gate_share(a)
                gate_softmax(a)
                if more:
                    keep_h0t(a + 1)
                gate_keep(a)
                add_experts(a, 0)
                norm2_front(b)
                add_experts(a, 1)
                norm2_back(b)
                x_max(b)
                x_step(b)
                x_scale(b)
                x_quantised(b)
                add_experts(a, 2)
                h_step(b)
                h_least(b)
                add_experts(a, 3)
                norm1_front(a)
                norm1_back(a)
                hidden(b, 0)
                h_size0(b)
                hidden(b, 1)
                h_scale(b)
                round_h0(b)
                quantise_h(b, 0)
                quantise_h(b, 1)
                y_step(b)
                if more:
                    row_max(a + 1, 0, 0)
                    row_max(a + 1, 0, 1)
                    row_max(a + 1, 0, 2)
                norm3(b)

            def ternary_sum(i, name):
                dve.wait_ge(w_in[name], 16)
                nc.vector.tensor_reduce(wabs[:, i:i + 1], ff_raw[i], AX.X, ALU.add, apply_absolute_value=True).then_inc(wabs_ready, 1)

            def ternary_sizes():
                dve.wait_ge(wsum_full, 1)
                nc.vector.tensor_scalar(wmean[:, :], bank_of("B", "s1")[:, 0:3], 1.0 / (D * FF), EPS, ALU.mult, ALU.max).then_inc(wmean_ready, 1)
                dve.wait_ge(wmean_ready, 1)
                nc.vector.reciprocal(winv[:, :], wmean[:, :]).then_inc(winv_ready, 1)
                nc.vector.tensor_tensor(gu_sq[:, :], wmean[:, 0:1], wmean[:, 0:1], ALU.mult).then_inc(gu_sq_ready, 1)
                dve.wait_ge(gu_sq_ready, 1)
                nc.vector.tensor_tensor(gu_size[:, :], gu_sq[:, :], wmean[:, 1:2], ALU.mult).then_inc(gu_size_ready, 1)

            def ternary_keep(i):
                turn = (1, 2, 0).index(i) + 1
                dve.wait_ge(wround, turn)
                nc.vector.tensor_scalar(ff_raw[i], ff_raw[i], ROUND + 1.0, ROUND - 1.0, ALU.min, ALU.max).then_inc(wclip, 1)
                dve.wait_ge(wclip, turn)
                if i > 0:
                    nc.vector.tensor_scalar(wq[:, i, :], ff_raw[i], ROUND, None, ALU.subtract).then_inc(wq_ready, 1)

            dve.wait_ge(w_in["const"], 64)
            for k in range(KD):
                nc.vector.tensor_scalar(pos_t[:, k, 1:S], pos_t[:, k, 1:S], tokb_t[:, k:k + 1], None, ALU.add).then_inc(pos_ready, 1)
                nc.vector.tensor_scalar(pos_t[:, k, 0:1], pos_t[:, k, 0:1], cls_t[:, k:k + 1], None, ALU.add).then_inc(pos_ready, 1)
            nc.vector.tensor_copy(ident_b[:, :], ident).then_inc(tables_ready, 1)
            nc.vector.tensor_copy(before_b[:, :], before_f).then_inc(tables_ready, 1)
            nc.vector.memset(magic_t[:, :], ROUND).then_inc(tables_ready, 1)
            nc.vector.memset(mhalf[:, :], -0.5).then_inc(tables_ready, 1)
            nc.vector.memset(v0[:, :, D0:D0 + 1], 1.0)
            dve.wait_ge(pos_ready, 2 * KD)
            stage_a(0)
            dve.wait_ge(gu_size_ready, 1)
            dve.wait_ge(wq_ready, 2)
            nc.vector.memset(v1[:, :, D1:D1 + 1], 1.0)
            both(1, 0)
            with dve.Fori(2, NG - 1) as g:
                both(g, g - 1)
            both(NG - 1, NG - 2, more=False)
            stage_b(NG - 1)

        @block.gpsimd
        def _(pool):
            def deviation(g, i):
                pool.wait_ge(ln_var[i], g + 1)
                pool.nop(nofuse=True)
                nc.gpsimd.tensor_scalar(var_eps[:, i:i + 1], mv[:, i, 1:2], EPS, None, ALU.add).then_inc(ln_shift[i], 1)
                pool.wait_ge(ln_shift[i], g + 1)
                nc.gpsimd.tensor_tensor(rstd[:, i:i + 1], var_eps[:, i:i + 1], mhalf[0:GT, :], ALU.pow).then_inc(ln_rstd[i], 1)

            def low_part(g, kind, lo, hi, whole, ready):
                pool.wait_ge(drained[kind], g + 1)
                nc.gpsimd.tensor_tensor(lo[:, :, :], whole[:, :, :], hi[:, :, :].bitcast(F32), ALU.subtract).then_inc(ready, 1)

            def h0t_split(g):
                pool.wait_ge(drained["tok"], g + 1)
                pool.nop(nofuse=True)
                nc.gpsimd.tensor_copy(h0t_hi[:, :, :], h0t[:, :, :]).then_inc(h0t_hi_ready, 1)
                pool.wait_ge(h0t_hi_ready, g + 1)
                nc.gpsimd.tensor_tensor(h0t_lo[:, :, :], h0t[:, :, :], h0t_hi[:, :, :].bitcast(F32), ALU.subtract).then_inc(h0t_parts, 1)

            def turn(a, b, more=True):
                deviation(a, 0)
                low_part(a, "h1t", h1t_lo, h1t_hi, h1t, h1t_parts)
                if more:
                    h0t_split(a + 1)
                if b is not None:
                    deviation(b, 2)
                deviation(a, 1)
                low_part(a, "h2t", h2t_lo, h2t_hi, h2t, h2t_parts)
                if b is not None:
                    deviation(b, 3)

            nc.gpsimd.memset(ones[:, :], 1.0).then_inc(ones_ready, 1)
            pool.wait_ge(tables_ready, 4)
            h0t_split(0)
            turn(0, None)
            pool.wait_ge(part_hi, 6)
            nc.gpsimd.tensor_tensor(o1w_part[1][:, :], o1w_raw, o1w_part[0][:, :].bitcast(F32), ALU.subtract).then_inc(o1w_lo_ready, 1)
            pool.wait_ge(wclip, 3)
            nc.gpsimd.tensor_scalar(wq[:, 0, :], gate_raw, ROUND, None, ALU.subtract).then_inc(gate_q_ready, 1)
            with pool.Fori(1, NG - 1) as g:
                turn(g, g - 1)
            turn(NG - 1, NG - 2, more=False)
            deviation(NG - 1, 2)
            deviation(NG - 1, 3)


_ORDER = ["xp", "consts", "pos", "cls", "tokb", "tokw", "qk0w", "v0w", "o0w", "wr", "we", "qk1w", "v1w", "o1w", "wg", "wu", "wd"]


def kernel(**inputs):
    import concourse.bacc as _bacc
    from concourse.bass_utils import run_bass_kernel_spmd as _run

    a = {k: np.asarray(v) for k, v in inputs.items()}

    def rows(w, k):
        return np.ascontiguousarray(w.reshape(k, 128, -1).transpose(1, 0, 2))

    patches = a["x"].reshape(B, CH, PER_SIDE, PATCH, PER_SIDE, PATCH).transpose(0, 2, 4, 1, 3, 5).reshape(B, S - 1, PD)
    xs = np.zeros((NG * IMG, S, PD), patches.dtype)
    xs[:B, 1:] = patches
    xp = xs.reshape(NG, GT, KP, 128).transpose(0, 3, 2, 1)

    t = np.arange(GT)
    same = t[:, None] // S == t[None, :] // S
    consts = np.zeros((128, 128 + 2 * GT + 2 + E), np.float32)
    consts[:, 0:128] = np.eye(128)
    consts[:GT, 128:128 + GT] = np.where(same & (t[None, :] <= t[:, None]), 0.0, MASKED)
    consts[:GT, 128 + GT:128 + 2 * GT] = same & (t[:, None] < t[None, :])
    p = np.arange(128)
    for par in range(2):
        consts[:, 128 + 2 * GT + par] = np.where(p // D0 % 2 == par, D0 ** -0.5, 0.0)
    consts[:, 130 + 2 * GT:] = np.arange(E)

    heads0 = [4 * j + 2 * t_ + par for t_ in range(2) for j in range(4) for par in range(2)]
    cols0 = np.concatenate([np.arange(h * D0, (h + 1) * D0) for h in heads0])
    qk0 = np.concatenate([a["L0_attn_q_heads"].T[:, cols0], a["L0_attn_k_heads"].T[:, cols0]], 1)
    def pair(w, half):
        w = w.transpose(2, 0, 1)
        order = [8 * half + i + 4 * z for i in range(4) for z in range(2)]
        return w[:, order, :].reshape(D, -1)
    q, k = a["L1_attn_w_q"], a["L1_attn_w_k"]
    qk1 = np.concatenate([pair(q, 0), pair(k, 0), pair(q, 1), pair(k, 1)], 1)

    data = {
        "xp": xp, "consts": consts,
        "pos": a["L0_tok_pos_embedding"].reshape(S, KD, 128).transpose(2, 1, 0),
        "cls": a["L0_tok_cls_token"].reshape(KD, 128).T,
        "tokb": a["L0_tok_b"].reshape(KD, 128).T,
        "tokw": rows(a["L0_tok_W"].T, KP),
        "qk0w": rows(qk0, KD),
        "v0w": rows(a["L0_attn_v_heads"].T, KD).reshape(128, -1),
        "o0w": rows(a["L0_attn_output_proj"].T, KD).reshape(128, -1),
        "wr": rows(a["L0_ffn_Wr"].T, KD),
        "we": rows(a["L0_ffn_We"].transpose(1, 0, 2).reshape(D, E * D), KD).reshape(128, -1),
        "qk1w": rows(qk1, KD),
        "v1w": rows(a["L1_attn_w_v"].transpose(2, 0, 1).reshape(D, W1), KD).reshape(128, -1),
        "o1w": rows(a["L1_attn_w_o"], KO).reshape(128, -1),
        "wg": rows(a["L1_ffn_w_gate"].T, KD).reshape(128, -1),
        "wu": rows(a["L1_ffn_w_up"].T, KD).reshape(128, -1),
        "wd": rows(a["L1_ffn_w_down"].T, KF).reshape(128, -1),
    }
    nc = _bacc.Bacc("TRN2", target_bir_lowering=False, num_devices=1)
    arrays, args = {}, []
    for name in _ORDER:
        v = np.ascontiguousarray(data[name])
        arrays[f"in_{name}"] = v
        args.append(nc.dram_tensor(f"in_{name}", v.shape, mybir.dt.from_np(v.dtype), kind="ExternalInput").ap())
    out = nc.dram_tensor("tokens_out", (NG, GT, D), F32, kind="ExternalOutput").ap()
    vit_tower(nc, *args, out)
    r = _run(nc, [arrays], core_ids=[0])
    return r.results[0]["tokens_out"].reshape(NG * IMG, S, D)[:B]
```
